# Optimizing a Trainium2 kernel written in Bass

```python
import numpy as np
import jax
import jax.numpy as jnp

def _softmax(x, axis=-1):
    return jax.nn.softmax(x, axis=axis)

def _gelu(x):
    return jax.nn.gelu(x, approximate=True)

def _silu(x):
    return jax.nn.silu(x)

def _sigmoid(x):
    return jax.nn.sigmoid(x)

def _layernorm(x, axis=-1, eps=1e-05):
    m = jnp.mean(x, axis=axis, keepdims=True)
    v = jnp.var(x, axis=axis, keepdims=True)
    return (x - m) / jnp.sqrt(v + eps)

def _scatter_add(tgt, idx, src, axis=0):
    return tgt.at[idx].add(src)

def _segment_sum(src, seg, n):
    return jax.ops.segment_sum(src, seg, n)
kernel_name = 'mk_adj_preln_d1_adj_r2_c385c8'

def setup_inputs(seed: int=0):
    np.random.seed(seed)
    _w = jnp.asarray

    def _rec_inputs():
        import jax
        import jax.numpy as jnp
        _gk = jax.random.key(seed)
        x = -0.000929 + 1 * jax.random.normal(jax.random.fold_in(_gk, 1), (8192, 128), jnp.float32)
        _a = jax.random.bernoulli(jax.random.fold_in(_gk, 2), 0.000488281, (8192, 8192))
        adj = _a.astype(jnp.int32)
        return (x, adj)
    x, adj = _rec_inputs()

    def _L0_gnn_setup():
        import jax, jax.numpy as jnp
        import numpy as np
        N = 4096
        IN = 128
        OUT = 128
        THR = 0.0001
        ALPHA = 0.2
        NEG = -1000000000.0
        key = jax.random.key(seed)
        k1, k2, k3, k4 = jax.random.split(key, 4)
        inp = jax.random.normal(k1, (N, IN), jnp.float32)
        W = jax.random.normal(k2, (IN, OUT), jnp.float32) * (1.414 * np.sqrt(2.0 / (IN + OUT)))
        a = jax.random.normal(k3, (2 * OUT, 1), jnp.float32) * (1.414 * np.sqrt(2.0 / (2 * OUT + 1)))
        adj = jax.random.randint(k4, (N, N), 0, 2, jnp.int32)
        return {'input': inp, 'W': W, 'a': a, 'adj': adj, 'M': N}
    _L0_gnn_all = _L0_gnn_setup()
    _L0_gnn_in = {k: v for k, v in _L0_gnn_all.items() if k in ('W', 'a')}
    del _L0_gnn_all
    return {'x': x, 'adj': adj, 'L0_gnn_W': _L0_gnn_in['W'], 'L0_gnn_a': _L0_gnn_in['a']}

def reference(x, adj, L0_gnn_W, L0_gnn_a):
    import jax
    import jax.numpy as jnp

    def _L0_gnn_ref(input, W, a, adj, M):
        import jax, jax.numpy as jnp
        import numpy as np
        N = 4096
        IN = 128
        OUT = 128
        THR = 0.0001
        ALPHA = 0.2
        NEG = -1000000000.0
        h = input @ W
        a_src = a[:OUT, 0]
        a_dst = a[OUT:, 0]
        e = jax.nn.leaky_relu((h[:M] @ a_src)[:, None] + (h @ a_dst)[None, :], negative_slope=ALPHA)
        valid = (adj[:M] > 0) & (h.sum(axis=1) != 0)[None, :]
        att = jax.nn.softmax(jnp.where(valid, e, NEG), axis=1)
        att = jnp.where(valid, att, 0.0)
        L = valid.sum(axis=1).astype(h.dtype)
        top = att.max(axis=1)
        attention = jnp.where(att >= THR, att, 0.0) * L[:, None]
        attention = jnp.where((top > THR)[:, None], attention, 0.0)
        h_prime = attention @ h
        return jax.nn.elu(h[:M] + h_prime)
    h = jnp.maximum(_layernorm(x, axis=-1), 0.0)
    x = x + _L0_gnn_ref(h, L0_gnn_W, L0_gnn_a, adj, 8192)
    return x

_drawn_inputs = setup_inputs


def setup_inputs(seed=0):
    import zlib

    import numpy as np

    out = dict(_drawn_inputs(seed))
    spreads = {}
    factors = {}
    for name, (base, spread) in spreads.items():
        noise = np.random.default_rng([zlib.crc32(name.encode()), seed]).standard_normal(out[name].shape)
        drawn = base * np.exp(spread * noise) if base else spread * noise
        out[name] = jnp.asarray(drawn.astype(out[name].dtype))
    for name, factor in factors.items():
        out[name] = (out[name] * factor).astype(out[name].dtype)
    return out
```

```python
from contextlib import ExitStack

import concourse.bass as bass
from concourse import mybir

F32 = mybir.dt.float32
BF16 = mybir.dt.bfloat16
I32 = mybir.dt.int32
ALU = mybir.AluOpType
ACT = mybir.ActivationFunctionType
AX_X = mybir.AxisListType.X

P = 128
EPS = 1e-5
THR = 1e-4
ALPHA = 0.2
BIG = 1e30
FLOOR = -1e29

BITS = 8
SEG = 128
SLOTS = 16
ALWAYS = 9
SECTIONS = ((9, 10), (10, 12), (12, 16))
CHUNKS = 2
XPARTS = 4
UNIT = 4


class Steps:

    def __init__(self, eng, sem):
        self.eng, self.sem, self.n = eng, sem, 0

    def did(self, ins):
        self.n += 1
        ins.then_inc(self.sem, 1)

    def wait(self, back=0):
        self.eng.wait_ge(self.sem, self.n - back)

    def restart(self):
        self.wait()
        self.eng.sem_clear(self.sem)
        self.n = 0


def wait_alone(eng, sem, value, waits):
    eng.wait_ge(sem, value)
    eng.sem_inc(waits, 1)


def gat_kernel(nc, x, adj, W, a, out, table, trow):
    N, D = x.shape
    TILES = N // P
    PAIRS = TILES // 2
    GROUPS = N // BITS
    NSEG = GROUPS // SEG
    CW = N // CHUNKS
    TW = table.shape[1]
    TCOL, FCOL = D, D + 1
    PART = TILES // XPARTS
    UNITS = TILES // UNIT
    BIAS = float((2 ** BITS - 1) * GROUPS // 2)
    S2 = 2 * SLOTS

    x_t = x.rearrange("(t p) d -> p t d", p=P)
    out_t = out.rearrange("(t p) d -> p t d", p=P)
    adj_t = adj.rearrange("(t p) j -> p t j", p=P)
    table_t = table.rearrange("(t p) d -> p t d", p=P)

    with ExitStack() as ctx:
        def sb(name, shape, dt):
            return ctx.enter_context(nc.sbuf_tensor(name, shape, dt))

        def ps(name, shape, dt):
            return ctx.enter_context(nc.psum_tensor(name, shape, dt))

        def sem(name):
            return ctx.enter_context(nc.semaphore(name))

        adj_sb = sb("adj_sb", [P, 2 * CHUNKS, CW], I32)
        mask = sb("mask", [P, 2 * CHUNKS, CW], BF16)
        gath = sb("gath", [P, 2, S2, TW], F32)
        h_all = sb("h_all", [P, TILES, TW], F32)
        x_all = gath[:, :, :, :].rearrange("p a b c -> p (a b c)")[:, 0:TILES * D].rearrange(
            "p (t d) -> p t d", d=D)
        gath_tail = gath[:, :, :, :].rearrange("p a b c -> p (a b c)")[:, TILES * D:2 * S2 * TW]
        sq_all = mask[:, :, :].rearrange("p a b -> p (a b)").bitcast(F32).rearrange("p (t d) -> p t d", d=D)

        d_adj = adj_sb[:, 0:CHUNKS, :].rearrange("p c w -> p (c w)")
        d_valid = d_adj.bitcast(F32)
        d_att = adj_sb[:, CHUNKS:2 * CHUNKS, :].rearrange("p c w -> p (c w)").bitcast(F32)
        t_row = mask[:, :, :].rearrange("p c w -> p (c w)").bitcast(F32)
        flag_row = gath[:, :, :, :].rearrange("p a b c -> p (a b c)")[:, 0:N]
        missed = sb("missed", [P, 4], F32)
        missed_b = sb("missed_b", [P, 1], BF16)
        redo_i = sb("redo_i", [1, 1], I32)
        cols = sb("cols", [P, 2, TILES], F32)
        rows = sb("rows", [TILES, 2, P], F32)
        one = sb("one", [P, 10], F32)

        ident = sb("ident", [P, P], F32)
        pack_w = sb("pack_w", [P, BITS, P], BF16)
        ones_b = sb("ones_b", [P, P], BF16)
        word_no = sb("word_no", [P, GROUPS], BF16)
        bit_mask = sb("bit_mask", [P, BITS], I32)
        bit_base = sb("bit_base", [P, BITS], I32)

        minus_half = sb("minus_half", [P, 1], F32)

        w_ext = sb("w_ext", [P, D + 3], F32)
        wT = sb("wT", [P, D], F32)
        a3 = sb("a3", [P, 3], F32)
        hn = sb("hn", [P, 2, UNIT, D], F32)
        hnT = sb("hnT", [P, 2, UNIT, P], F32)
        s_all = sb("s_all", [P, TILES], F32)
        mean = sb("mean", [P, TILES], F32)
        var = sb("var", [P, TILES], F32)
        std = sb("std", [P, TILES], F32)
        rstd = sb("rstd", [P, TILES], F32)
        sum1 = sb("sum1", [P, TILES], F32)

        cand = sb("cand", [P, 2, NSEG * 8], F32)
        cand2 = sb("cand2", [P, 2, NSEG * 8], F32)
        words = sb("words", [P, S2], F32)
        words_i = sb("words_i", [P, S2], I32)
        word_n = sb("word_n", [P, S2], I32)
        bits = sb("bits", [P, S2, BITS], I32)
        keyf = sb("keyf", [P, S2, BITS], F32)
        ekey = sb("ekey", [P, S2, BITS], F32)
        ekey2 = sb("ekey2", [P, S2, BITS], F32)
        keys = sb("keys", [P, 2, S2], F32)
        idx = sb("idx", [P, 2, S2], I32)
        has = sb("has", [P, 2, S2], BF16)
        found = sb("found", [P, S2], F32)
        cnt_i = sb("cnt_i", [1, 2, S2], I32)
        sgn_sum = sb("sgn_sum", [P, TILES * CHUNKS], F32)

        valid = sb("valid", [P, S2], F32)
        deg = sb("deg", [P, 2], F32)
        tm = sb("tm", [P, S2], F32)
        tm2 = sb("tm2", [P, S2], F32)
        mx = sb("mx", [P, 4, 2], F32)
        sc = sb("sc", [P, 3, S2], F32)
        prob = sb("prob", [P, S2], F32)
        zz = sb("zz", [P, 4, 2], F32)
        att = sb("att", [P, 3, S2], F32)
        zacc = sb("zacc", [P, 2, D], F32)
        neg = sb("neg", [P, 2, D], F32)
        eneg = sb("eneg", [P, 2, D], F32)
        rsum = sb("rsum", [P, 2, D], F32)
        xr = sb("xr", [P, 2, 2, D], F32)
        ob = sb("ob", [P, 2, 2, D], F32)

        ps_words = [ps(f"ps_words{i}", [P, GROUPS], F32) for i in range(2)]
        ps_ext = [ps(f"ps_ext{i}", [P, 512], F32) for i in range(2)]
        ps_cnt = ps("ps_cnt", [P, 512], F32)
        ps_misc = ps("ps_misc", [P, 512], F32)
        ps_T = [ps_words[0][:, i * 512:(i + 1) * 512].rearrange("p (t d) -> p t d", d=P) for i in range(2)]
        ps_H = [ps_words[1][:, i * 512:(i + 1) * 512].rearrange("p (t d) -> p t d", d=D) for i in range(2)]

        const_ready = sem("const_ready")
        pool_steps = sem("pool_steps")
        pool_waits = sem("pool_waits")
        dve_steps = sem("dve_steps")
        dve_waits = sem("dve_waits")
        x_landed = [sem(f"x_landed{i}") for i in range(XPARTS)]
        w_landed = sem("w_landed")
        adj_landed = [sem(f"adj_landed{i}") for i in range(2 * CHUNKS)]
        xc_ready = sem("xc_ready")
        sq_ready = sem("sq_ready")
        var_ready = sem("var_ready")
        std_ready = sem("std_ready")
        wT_psum = sem("wT_psum")
        wT_ready = sem("wT_ready")
        we_psum = sem("we_psum")
        we_ready = sem("we_ready")
        hn_ready = sem("hn_ready")
        hnT_psum = sem("hnT_psum")
        hnT_ready = sem("hnT_ready")
        h_psum = sem("h_psum")
        h_ready = sem("h_ready")
        table_stored = sem("table_stored")
        mask_ready = sem("mask_ready")
        mask_used = sem("mask_used")
        words_ready = sem("words_ready")
        words_used = sem("words_used")
        idx_ready = sem("idx_ready")
        has_ready = sem("has_ready")
        cnt_psum = sem("cnt_psum")
        cnt_ready = sem("cnt_ready")
        gathered = [sem(f"gathered{i}") for i in range(2)]
        score_ready = sem("score_ready")
        prob_ready = sem("prob_ready")
        neg_ready = sem("neg_ready")
        eneg_ready = sem("eneg_ready")
        xr_landed = [sem(f"xr_landed{i}") for i in range(2)]
        out_ready = sem("out_ready")
        out_stored = [sem(f"out_stored{i}") for i in range(2)]

        missed_ready = sem("missed_ready")
        redo_psum = sem("redo_psum")
        redo_ready = sem("redo_ready")
        cols_ready = sem("cols_ready")
        rows_psum = sem("rows_psum")
        rows_ready = sem("rows_ready")
        rows_stored = sem("rows_stored")
        rows_landed = sem("rows_landed")
        d_free = sem("d_free")
        d_adj_landed = sem("d_adj_landed")
        d_x_landed = sem("d_x_landed")
        d_score_ready = sem("d_score_ready")
        d_prob_ready = sem("d_prob_ready")
        d_att_ready = sem("d_att_ready")
        d_stage_ready = sem("d_stage_ready")
        d_T_psum = sem("d_T_psum")
        d_T_ready = sem("d_T_ready")
        d_acc_psum = sem("d_acc_psum")
        d_neg_ready = sem("d_neg_ready")
        d_eneg_ready = sem("d_eneg_ready")
        d_out_ready = sem("d_out_ready")
        d_stored = sem("d_stored")
        GROUPS_D = TILES // UNIT
        stage, attT = hn[:, 0, :, :], hnT[:, 0, :, :]
        ps_DT = ps_T[0]
        ps_acc = ps_words[1][:, 0:D]

        def must_redo(eng):
            eng.wait_ge(redo_ready, 1)
            return eng.value_load(redo_i[0:1, 0:1], min_val=0, max_val=P) > 0

        block = ctx.enter_context(nc.Block())

        @block.sync
        def _(sp):
            def load_adj(i, par):
                q = 2 * i + par
                for b in range(2 * CHUNKS):
                    ti, c = b // CHUNKS, b % CHUNKS
                    if not (isinstance(q, int) and q == 0):
                        sp.wait_ge(mask_ready, 2 * CHUNKS * q + (b + 1 - 2 * CHUNKS))
                    sp.dma_start(adj_sb[:, b, :], adj_t[:, bass.ds(2 * q + ti, 1), c * CW:(c + 1) * CW]
                                 ).then_inc(adj_landed[b], 16)

            def load_x(i, par):
                q = 2 * i + par
                if not (isinstance(i, int) and i == 0):
                    sp.wait_ge(out_ready, q - 1)
                sp.dma_start(xr[:, par, :, :], x_t[:, bass.ds(2 * q, 2), :]).then_inc(xr_landed[par], 16)

            def store(i, par):
                q = 2 * i + par
                sp.wait_ge(out_ready, q + 1)
                sp.dma_start(out_t[:, bass.ds(2 * q, 2), :], ob[:, par, :, :]).then_inc(out_stored[par], 16)

            for k in range(XPARTS):
                sp.dma_start(x_all[:, k * PART:(k + 1) * PART, :], x_t[:, k * PART:(k + 1) * PART, :]
                             ).then_inc(x_landed[k], 16)
                if k == 0:
                    sp.dma_start(w_ext[:, 0:D], W).then_inc(w_landed, 16)
                    sp.dma_start(a3[:, 0:1], a[D:2 * D, :]).then_inc(w_landed, 16)
                    sp.dma_start(a3[:, 2:3], a[0:D, :]).then_inc(w_landed, 16)
            load_adj(0, 0)
            sp.wait_ge(const_ready, 2)
            for k in range(XPARTS):
                sp.wait_ge(h_ready, (k + 1) * UNITS // XPARTS)
                sp.dma_start(table_t[:, k * PART:(k + 1) * PART, :], h_all[:, k * PART:(k + 1) * PART, :]
                             ).then_inc(table_stored, 16)
            load_adj(0, 1)
            load_adj(1, 0)
            load_x(0, 0)
            load_adj(1, 1)
            load_x(0, 1)
            store(0, 0)
            with sp.Fori(2, PAIRS // 2) as i:
                for par in range(2):
                    load_adj(i, par)
                    load_x(i - 1, par)
                    store(i - 2 + par, 1 - par)
            load_x(PAIRS // 2 - 1, 0)
            store(PAIRS // 2 - 2, 1)
            load_x(PAIRS // 2 - 1, 1)
            store(PAIRS // 2 - 1, 0)
            store(PAIRS // 2 - 1, 1)
            for par in range(2):
                sp.wait_ge(out_stored[par], 16 * (PAIRS // 2))

            with sp.If(must_redo(sp)):
                sp.wait_ge(rows_ready, 1)
                for r in range(2):
                    sp.dma_start(trow[r:r + 1, :].rearrange("a (c p) -> (a c) p", p=P), rows[:, r, :]
                                 ).then_inc(rows_stored, 16)
                sp.wait_ge(rows_stored, 32)
                sp.dma_start(t_row, trow[0:1, :].to_broadcast([P, N])).then_inc(rows_landed, 16)
                sp.dma_start(flag_row, trow[1:2, :].to_broadcast([P, N])).then_inc(rows_landed, 16)
                with sp.Fori(0, TILES) as t:
                    sp.wait_ge(d_free, t + 1)
                    sp.dma_start(d_adj, adj_t[:, bass.ds(t, 1), :].rearrange("p a j -> p (a j)")
                                 ).then_inc(d_adj_landed, 16)
                    sp.dma_start(xr[:, 0, 0:1, :], x_t[:, bass.ds(t, 1), :]).then_inc(d_x_landed, 16)
                    sp.wait_ge(d_out_ready, t + 1)
                    sp.dma_start(out_t[:, bass.ds(t, 1), :], ob[:, 0, 0:1, :]).then_inc(d_stored, 16)
                sp.wait_ge(d_stored, 16 * TILES)

        @block.gpsimd
        def _(pool):
            st = Steps(pool, pool_steps)

            def made(ins):
                st.did(ins)
                st.wait()

            made(nc.gpsimd.memset(a3[:, 1:2], 1.0))
            made(nc.gpsimd.memset(ident[:, :], 0.0))
            made(nc.gpsimd.affine_select(out=ident[:, :], in_=ident[:, :], compare_op=ALU.not_equal, fill=1.0,
                                         base=0, pattern=[[-1, P]], channel_multiplier=1))
            made(nc.gpsimd.memset(minus_half[:, :], -0.5))
            pool.sem_inc(const_ready, 1)
            made(nc.gpsimd.memset(pack_w[:, :, :], 0.0))
            for b in range(BITS):
                made(nc.gpsimd.affine_select(out=pack_w[:, b, :], in_=pack_w[:, b, :], compare_op=ALU.not_equal,
                                             fill=float(2 ** b * GROUPS // 2), base=0, pattern=[[-1, P]],
                                             channel_multiplier=1))
            made(nc.gpsimd.memset(ones_b[:, :], 1.0))
            made(nc.gpsimd.memset(word_no[:, :], 0.0))
            hi = GROUPS // P
            made(nc.gpsimd.iota(word_no[0:1, :].rearrange("p (h l) -> p h l", l=P), [[-P, hi], [0, P]],
                                base=GROUPS - P, channel_multiplier=0, allow_small_or_imprecise_dtypes=True))
            made(nc.gpsimd.iota(word_no[32:33, :].rearrange("p (h l) -> p h l", l=P), [[0, hi], [-1, P]],
                                base=P - 1, channel_multiplier=0, allow_small_or_imprecise_dtypes=True))
            for b in range(BITS):
                made(nc.gpsimd.memset(bit_mask[:, b:b + 1], GROUPS * 2 ** b))
            made(nc.gpsimd.iota(bit_base[:, :], [[-GROUPS, BITS]], base=1 + GROUPS * (BITS - 1),
                                channel_multiplier=0))
            made(nc.gpsimd.memset(gath_tail, 0.0))
            made(nc.gpsimd.memset(h_all[:, :, FCOL + 1:TW], 0.0))
            pool.sem_inc(const_ready, 1)

            def gather(par, ti, k):
                s = ti * SLOTS + k
                nc.gpsimd.indirect_dma_start(
                    gath[:, par, s, :], None, table[:, :],
                    bass.IndirectOffsetOnAxis(ap=idx[:, par, s:s + 1], axis=0),
                    bounds_check=N - 1, oob_is_err=False).then_inc(gathered[par], 16)

            def pair(i, par):
                q = 2 * i + par
                if not (isinstance(i, int) and i == 0):
                    pool.wait_ge(neg_ready, q - 1)
                wait_alone(pool, idx_ready, q + 1, pool_waits)
                for k in range(ALWAYS):
                    for ti in range(2):
                        gather(par, ti, k)
                wait_alone(pool, cnt_ready, q + 1, pool_waits)
                for ti in range(2):
                    for lo, hi in SECTIONS:
                        users = pool.value_load(cnt_i[0:1, par, ti * SLOTS + lo:ti * SLOTS + lo + 1],
                                                min_val=0, max_val=P)
                        with pool.If(users > 0):
                            for k in range(lo, hi):
                                gather(par, ti, k)
                        with pool.Else():
                            pool.inc_swdge_sem([gathered[par]], [16 * (hi - lo)], mode="add")

            pool.wait_ge(table_stored, 16 * XPARTS)
            pair(0, 0)
            pair(0, 1)
            with pool.Fori(1, PAIRS // 2) as i:
                pair(i, 0)
                pair(i, 1)

        @block.scalar
        def _(act):
            act.wait_ge(const_ready, 1)
            for k in range(XPARTS):
                act.wait_ge(xc_ready, k + 1)
                nc.scalar.activation(sq_all[:, k * PART:(k + 1) * PART, :], x_all[:, k * PART:(k + 1) * PART, :],
                                     ACT.Square).then_inc(sq_ready, 1)
            act.wait_ge(var_ready, 1)
            nc.scalar.activation(std[:, :], var[:, :], ACT.Sqrt).then_inc(std_ready, 1)

            def copy_T(u, par, first):
                act.wait_ge(hnT_psum, u + 1)
                if not first:
                    act.wait_ge(h_psum, u - 1)
                nc.scalar.copy(hnT[:, par, :, :], ps_T[par]).then_inc(hnT_ready, 1)

            copy_T(0, 0, True)
            copy_T(1, 1, True)
            with act.Fori(1, UNITS // 2) as i:
                copy_T(2 * i, 0, False)
                copy_T(2 * i + 1, 1, False)

            def cast(i, par, b):
                q = 2 * i + par
                act.wait_ge(adj_landed[b], 16 * (q + 1))
                if not (isinstance(q, int) and q == 0):
                    act.wait_ge(mask_used, 2 * CHUNKS * q + (b + 1 - 2 * CHUNKS))
                nc.scalar.activation(mask[:, b, :], adj_sb[:, b, :], ACT.Sign, bias=minus_half[:, 0:1],
                                     accum_out=sgn_sum[:, bass.ds(2 * CHUNKS * q + b, 1)]
                                     ).then_inc(mask_ready, 1)

            def exp_scores(q):
                act.wait_ge(score_ready, q + 1)
                nc.scalar.activation(prob[:, :], sc[:, 2, :], ACT.Exp).then_inc(prob_ready, 1)

            def exp_neg(q):
                act.wait_ge(neg_ready, q + 1)
                nc.scalar.activation(eneg[:, :, :], neg[:, :, :], ACT.Exp).then_inc(eneg_ready, 1)

            def pair(i, par, lag):
                cast(i, par, 0)
                cast(i, par, 1)
                if lag:
                    exp_scores(2 * i + par - 2)
                cast(i, par, 2)
                cast(i, par, 3)
                if lag:
                    exp_neg(2 * i + par - 2)

            act.wait_ge(var_ready, 1)
            pair(0, 0, False)
            pair(0, 1, False)
            with act.Fori(1, PAIRS // 2) as i:
                pair(i, 0, True)
                pair(i, 1, True)
            for q in (PAIRS - 2, PAIRS - 1):
                exp_scores(q)
                exp_neg(q)

            with act.If(must_redo(act)):
                with act.Fori(0, TILES) as t:
                    act.wait_ge(d_score_ready, t + 1)
                    nc.scalar.activation(d_att, d_att, ACT.Exp, bias=one[:, 4:5], accum_out=one[:, 5:6]
                                         ).then_inc(d_prob_ready, 1)
                    act.wait_ge(d_att_ready, t + 1)
                    with act.Fori(0, GROUPS_D) as g:
                        act.wait_ge(d_T_psum, GROUPS_D * t + g + 1)
                        nc.scalar.copy(stage.rearrange("p t d -> p (t d)"), d_att[:, bass.ds(UNIT * P * g, UNIT * P)]
                                       ).then_inc(d_stage_ready, 1)
                    act.wait_ge(d_neg_ready, t + 1)
                    nc.scalar.activation(eneg[:, 0, :], neg[:, 0, :], ACT.Exp).then_inc(d_eneg_ready, 1)

        @block.tensor
        def _(pe):
            pe.wait_ge(const_ready, 1)
            pe.wait_ge(w_landed, 48)
            nc.tensor.transpose(ps_misc[:, 0:D], w_ext[:, 0:D], ident[:, :]).then_inc(wT_psum, 1)
            pe.wait_ge(wT_ready, 1)
            nc.tensor.matmul(ps_misc[:, D:D + 3], wT[:, :], a3[:, :], start=True, stop=True).then_inc(we_psum, 1)
            pe.wait_ge(we_ready, 1)

            def transposes(u, par, first):
                pe.wait_ge(hn_ready, u + 1)
                if not first:
                    pe.wait_ge(hnT_ready, u - 1)
                for t in range(UNIT):
                    last = nc.tensor.transpose(ps_T[par][:, t, :], hn[:, par, t, :], ident[:, :])
                last.then_inc(hnT_psum, 1)

            def project(u, par, first):
                pe.wait_ge(hnT_ready, u + 1)
                if not first:
                    pe.wait_ge(h_ready, u - 1)
                for t in range(UNIT):
                    nc.tensor.matmul(ps_H[par][:, t, :], hnT[:, par, t, :], w_ext[:, 0:D], start=True, stop=True)
                    last = nc.tensor.matmul(ps_ext[par][:, 4 * t:4 * t + 3], hnT[:, par, t, :],
                                            w_ext[:, D:D + 3], start=True, stop=True)
                last.then_inc(h_psum, 1)

            transposes(0, 0, True)
            transposes(1, 1, True)
            project(0, 0, True)
            transposes(2, 0, False)
            project(1, 1, True)
            with pe.Fori(1, UNITS // 2 - 1) as i:
                transposes(2 * i + 1, 1, False)
                project(2 * i, 0, False)
                transposes(2 * i + 2, 0, False)
                project(2 * i + 1, 1, False)
            transposes(UNITS - 1, 1, False)
            project(UNITS - 2, 0, False)
            project(UNITS - 1, 1, False)
            pe.wait_ge(h_ready, UNITS)
            pe.wait_ge(const_ready, 2)

            def pack(i, par, ti):
                q = 2 * i + par
                if not (isinstance(q, int) and q == 0):
                    pe.wait_ge(words_used, 2 * q + ti - 1)
                for c in range(CHUNKS):
                    b = ti * CHUNKS + c
                    pe.wait_ge(mask_ready, 2 * CHUNKS * q + b + 1)
                    per = BITS // CHUNKS
                    for bit in range(per):
                        for bank in range(GROUPS // 512):
                            last = nc.tensor.matmul(
                                ps_words[ti][:, bank * 512:(bank + 1) * 512], pack_w[:, c * per + bit, :],
                                mask[:, b, bit * GROUPS + bank * 512:bit * GROUPS + (bank + 1) * 512],
                                start=(c == 0 and bit == 0), stop=False)
                    last.then_inc(mask_used, 1)
                for bank in range(GROUPS // 512):
                    last = nc.tensor.matmul(ps_words[ti][:, bank * 512:(bank + 1) * 512], ones_b[:, :],
                                            word_no[:, bank * 512:(bank + 1) * 512], start=False, stop=True)
                last.then_inc(words_ready, 1)

            def pair(i, par):
                pack(i, par, 0)
                pack(i, par, 1)
                pe.wait_ge(has_ready, 2 * i + par + 1)
                nc.tensor.matmul(ps_cnt[0:1, par * S2:(par + 1) * S2], ones_b[:, 0:1], has[:, par, :],
                                 start=True, stop=True).then_inc(cnt_psum, 1)

            pair(0, 0)
            pair(0, 1)
            with pe.Fori(1, PAIRS // 2) as i:
                pair(i, 0)
                pair(i, 1)

            pe.wait_ge(missed_ready, 1)
            nc.tensor.matmul(ps_cnt[0:1, 2 * S2:2 * S2 + 1], ones_b[:, 0:1], missed_b[:, :], start=True, stop=True
                             ).then_inc(redo_psum, 1)
            with pe.If(must_redo(pe)):
                pe.wait_ge(cols_ready, 1)
                for r in range(2):
                    last = nc.tensor.transpose(ps_misc[0:TILES, r * P:(r + 1) * P], cols[:, r, :], ident[:, :])
                last.then_inc(rows_psum, 1)
                pe.sem_inc(d_T_psum, 1)

                def group(t, g, start, stop):
                    pe.wait_ge(d_stage_ready, GROUPS_D * t + g + 1)
                    for k in range(UNIT):
                        last = nc.tensor.transpose(ps_DT[:, k, :], stage[:, k, :], ident[:, :])
                    last.then_inc(d_T_psum, 1)
                    pe.wait_ge(d_T_ready, GROUPS_D * t + g + 1)
                    for k in range(UNIT):
                        last = nc.tensor.matmul(
                            ps_acc, attT[:, k, :], h_all[:, bass.ds(UNIT * g + k, 1), 0:D].rearrange("p a d -> p (a d)"),
                            start=start and k == 0, stop=stop and k == UNIT - 1)
                    last.then_inc(d_acc_psum, 1)

                with pe.Fori(0, TILES) as t:
                    group(t, 0, True, False)
                    with pe.Fori(1, GROUPS_D - 1) as g:
                        group(t, g, False, False)
                    group(t, GROUPS_D - 1, False, True)

        @block.vector
        def _(dve):
            st = Steps(dve, dve_steps)
            dve.wait_ge(wT_psum, 1)
            nc.vector.tensor_copy(wT[:, :], ps_misc[:, 0:D]).then_inc(wT_ready, 1)
            dve.wait_ge(we_psum, 1)
            nc.vector.tensor_copy(w_ext[:, D:D + 3], ps_misc[:, D:D + 3]).then_inc(we_ready, 1)

            for k in range(XPARTS):
                part = slice(k * PART, (k + 1) * PART)
                dve.wait_ge(x_landed[k], 16)
                st.did(nc.vector.reduce_sum(sum1[:, part], x_all[:, part, :], AX_X))
                st.wait()
                st.did(nc.vector.tensor_scalar(mean[:, part], sum1[:, part], 1.0 / D, None, ALU.mult))
                st.wait()
                nc.vector.tensor_tensor(x_all[:, part, :], x_all[:, part, :],
                                        mean[:, part].unsqueeze(2).to_broadcast([P, PART, D]),
                                        ALU.subtract).then_inc(xc_ready, 1)
            for k in range(XPARTS):
                part = slice(k * PART, (k + 1) * PART)
                dve.wait_ge(sq_ready, k + 1)
                st.did(nc.vector.reduce_sum(sum1[:, part], sq_all[:, part, :], AX_X))
            st.wait()
            nc.vector.tensor_scalar(var[:, :], sum1[:, :], 1.0 / D, EPS, ALU.mult, ALU.add).then_inc(var_ready, 1)
            dve.wait_ge(std_ready, 1)
            st.did(nc.vector.reciprocal(rstd[:, :], std[:, :]))
            st.wait()

            def normalise(u, par, first):
                if not first:
                    dve.wait_ge(hnT_psum, u - 1)
                nc.vector.scalar_tensor_tensor(
                    out=hn[:, par, :, :], in0=x_all[:, bass.ds(UNIT * u, UNIT), :], scalar=0.0,
                    in1=rstd[:, bass.ds(UNIT * u, UNIT)].unsqueeze(2).to_broadcast([P, UNIT, D]),
                    op0=ALU.max, op1=ALU.mult).then_inc(hn_ready, 1)

            def keep_h(u, par):
                ext = ps_ext[par][:, 0:4 * UNIT].rearrange("p (t c) -> p t c", c=4)
                tiles = bass.ds(UNIT * u, UNIT)
                dve.wait_ge(h_psum, u + 1)
                nc.vector.tensor_copy(h_all[:, tiles, 0:D], ps_H[par])
                nc.vector.tensor_copy(h_all[:, tiles, TCOL:TCOL + 1], ext[:, :, 0:1])
                nc.vector.tensor_scalar(h_all[:, tiles, FCOL:FCOL + 1], ext[:, :, 1:2], 0.0, None, ALU.not_equal)
                nc.vector.tensor_copy(s_all[:, tiles].unsqueeze(2), ext[:, :, 2:3]).then_inc(h_ready, 1)

            normalise(0, 0, True)
            normalise(1, 1, True)
            keep_h(0, 0)
            with dve.Fori(1, UNITS // 2) as i:
                normalise(2 * i, 0, False)
                keep_h(2 * i - 1, 1)
                normalise(2 * i + 1, 1, False)
                keep_h(2 * i, 0)
            keep_h(UNITS - 1, 1)
            st.did(nc.vector.memset(found[:, :], 0.0))
            dve.wait_ge(const_ready, 2)

            def top16(out, first, rest, src, empty):
                st.did(nc.vector.max(out[:, 0:8], src))
                st.wait()
                st.did(nc.vector.match_replace(rest, out[:, 0:8], src, empty))
                st.wait()
                return nc.vector.max(out[:, 8:16], rest)

            def extract(i, par):
                q = 2 * i + par
                for ti in range(2):
                    wait_alone(dve, words_ready, 2 * q + ti + 1, dve_waits)
                    for s in range(NSEG):
                        st.did(nc.vector.max(cand[:, ti, s * 8:(s + 1) * 8],
                                             ps_words[ti][:, s * SEG:(s + 1) * SEG]))
                    st.wait()
                    dve.sem_inc(words_used, 1)
                    st.did(top16(words[:, ti * SLOTS:(ti + 1) * SLOTS], None, cand2[:, ti, :], cand[:, ti, :], -BIG))
                st.wait()
                st.did(nc.vector.tensor_scalar(words_i[:, :], words[:, :], BIAS, None, ALU.add))
                st.wait()
                st.did(nc.vector.tensor_scalar(word_n[:, :], words_i[:, :], GROUPS - 1, None, ALU.bitwise_and))
                st.did(nc.vector.tensor_tensor(bits[:, :, :], words_i[:, :].unsqueeze(2).to_broadcast([P, S2, BITS]),
                                               bit_mask[:, :].unsqueeze(1).to_broadcast([P, S2, BITS]),
                                               ALU.bitwise_and))
                st.wait(1)
                st.did(nc.vector.tensor_tensor(keyf[:, :, :], word_n[:, :].unsqueeze(2).to_broadcast([P, S2, BITS]),
                                               bit_base[:, :].unsqueeze(1).to_broadcast([P, S2, BITS]), ALU.add))
                st.wait()
                st.did(nc.vector.scalar_tensor_tensor(out=ekey[:, :, :], in0=bits[:, :, :], scalar=0.0,
                                                      in1=keyf[:, :, :], op0=ALU.is_gt, op1=ALU.mult))
                st.wait()
                for ti in range(2):
                    part = slice(ti * SLOTS, (ti + 1) * SLOTS)
                    st.did(top16(keys[:, par, part], None, ekey2[:, part, :].rearrange("p s b -> p (s b)"),
                                 ekey[:, part, :].rearrange("p s b -> p (s b)"), 0.0))
                st.wait()
                nc.vector.tensor_scalar(idx[:, par, :], keys[:, par, :], -1.0, float(N), ALU.mult, ALU.add
                                        ).then_inc(idx_ready, 1)
                nc.vector.tensor_scalar(has[:, par, :], keys[:, par, :], 0.0, None, ALU.is_gt).then_inc(has_ready, 1)
                dve.wait_ge(has_ready, q + 1)
                st.did(nc.vector.tensor_tensor(found[:, :], found[:, :], has[:, par, :], ALU.add))
                dve.wait_ge(cnt_psum, q + 1)
                nc.vector.tensor_copy(cnt_i[0:1, par, :], ps_cnt[0:1, par * S2:(par + 1) * S2]).then_inc(cnt_ready, 1)

            def per_tile(v):
                return v.unsqueeze(2).to_broadcast([P, 2, SLOTS])

            def by_tile(v):
                return v.rearrange("p (t k) -> p t k", k=SLOTS)

            def aggregate(i, par):
                q = 2 * i + par
                s_q = s_all[:, bass.ds(2 * q, 2)]
                dve.wait_ge(gathered[par], 16 * S2 * (i + 1))
                t_j, flag = gath[:, par, :, TCOL], gath[:, par, :, FCOL]
                st.did(nc.vector.scalar_tensor_tensor(out=valid[:, :], in0=keys[:, par, :], scalar=0.0, in1=flag,
                                                      op0=ALU.is_gt, op1=ALU.mult))
                st.wait()
                st.did(nc.vector.tensor_scalar(tm[:, :], valid[:, :], BIG, -BIG, ALU.mult, ALU.add))
                st.did(nc.vector.reduce_sum(deg[:, :], by_tile(valid[:, :]), AX_X))
                st.wait(1)
                st.did(nc.vector.tensor_tensor(tm2[:, :], tm[:, :], t_j, ALU.add))
                st.wait()
                st.did(nc.vector.reduce_max(mx[:, 0, :], by_tile(tm2[:, :]), AX_X))
                st.did(nc.vector.tensor_tensor(by_tile(sc[:, 0, :]), by_tile(tm2[:, :]), per_tile(s_q), ALU.add))
                st.wait(1)
                st.did(nc.vector.tensor_tensor(mx[:, 1, :], mx[:, 0, :], s_q, ALU.add))
                st.wait(1)
                st.did(nc.vector.scalar_tensor_tensor(out=sc[:, 1, :], in0=sc[:, 0, :], scalar=ALPHA,
                                                      in1=sc[:, 0, :], op0=ALU.mult, op1=ALU.max))
                st.wait(1)
                st.did(nc.vector.scalar_tensor_tensor(out=mx[:, 2, :], in0=mx[:, 1, :], scalar=ALPHA,
                                                      in1=mx[:, 1, :], op0=ALU.mult, op1=ALU.max))
                st.wait()
                st.did(nc.vector.tensor_scalar(mx[:, 3, :], mx[:, 2, :], FLOOR, None, ALU.max))
                st.wait()
                nc.vector.tensor_tensor(by_tile(sc[:, 2, :]), by_tile(sc[:, 1, :]), per_tile(mx[:, 3, :]),
                                        ALU.subtract).then_inc(score_ready, 1)
                dve.wait_ge(prob_ready, q + 1)
                st.did(nc.vector.reduce_sum(zz[:, 0, :], by_tile(prob[:, :]), AX_X))
                st.wait()
                st.did(nc.vector.tensor_scalar(zz[:, 1, :], zz[:, 0, :], 1.0 / BIG, None, ALU.max))
                st.wait()
                st.did(nc.vector.reciprocal(zz[:, 2, :], zz[:, 1, :]))
                st.wait()
                st.did(nc.vector.scalar_tensor_tensor(out=zz[:, 3, :], in0=zz[:, 2, :], scalar=THR, in1=deg[:, :],
                                                      op0=ALU.is_gt, op1=ALU.mult))
                st.did(nc.vector.tensor_tensor(by_tile(att[:, 0, :]), by_tile(prob[:, :]), per_tile(zz[:, 2, :]),
                                               ALU.mult))
                st.wait()
                st.did(nc.vector.scalar_tensor_tensor(out=att[:, 1, :], in0=att[:, 0, :], scalar=THR,
                                                      in1=att[:, 0, :], op0=ALU.is_ge, op1=ALU.mult))
                st.wait()
                st.did(nc.vector.tensor_tensor(by_tile(att[:, 2, :]), by_tile(att[:, 1, :]), per_tile(zz[:, 3, :]),
                                               ALU.mult))
                st.wait()
                for k in range(SLOTS):
                    for ti in range(2):
                        s = ti * SLOTS + k
                        if k == 0:
                            so_far = h_all[:, bass.ds(2 * q + ti, 1), 0:D].rearrange("p a d -> p (a d)")
                        else:
                            so_far = zacc[:, ti, :]
                            st.wait(1)
                        st.did(nc.vector.scalar_tensor_tensor(
                            out=zacc[:, ti, :], in0=gath[:, par, s, 0:D], scalar=att[:, 2, s:s + 1],
                            in1=so_far, op0=ALU.mult, op1=ALU.add))
                st.wait()
                nc.vector.tensor_scalar(neg[:, :, :], zacc[:, :, :], 0.0, None, ALU.min).then_inc(neg_ready, 1)
                dve.wait_ge(eneg_ready, q + 1)
                st.did(nc.vector.scalar_tensor_tensor(out=rsum[:, :, :], in0=zacc[:, :, :], scalar=0.0,
                                                      in1=eneg[:, :, :], op0=ALU.max, op1=ALU.add))
                dve.wait_ge(xr_landed[par], 16 * (i + 1))
                if not (isinstance(i, int) and i == 0):
                    dve.wait_ge(out_stored[par], 16 * i)
                st.wait()
                nc.vector.scalar_tensor_tensor(out=ob[:, par, :, :], in0=rsum[:, :, :], scalar=-1.0,
                                               in1=xr[:, par, :, :], op0=ALU.add, op1=ALU.add
                                               ).then_inc(out_ready, 1)

            extract(0, 0)
            extract(0, 1)
            aggregate(0, 0)
            st.restart()
            with dve.Fori(1, PAIRS // 2) as i:
                extract(i, 0)
                aggregate(i - 1, 1)
                extract(i, 1)
                aggregate(i, 0)
                st.restart()
            aggregate(PAIRS // 2 - 1, 1)
            st.restart()

            dve.wait_ge(mask_ready, 2 * CHUNKS * PAIRS)
            st.did(nc.vector.reduce_sum(missed[:, 0:1], sgn_sum[:, :], AX_X))
            st.did(nc.vector.reduce_sum(missed[:, 1:2], found[:, :], AX_X))
            st.wait(1)
            st.did(nc.vector.tensor_scalar(missed[:, 2:3], missed[:, 0:1], 0.5, float(TILES * N // 2), ALU.mult, ALU.add))
            st.wait()
            st.did(nc.vector.tensor_tensor(missed[:, 3:4], missed[:, 2:3], missed[:, 1:2], ALU.subtract))
            st.wait()
            nc.vector.tensor_scalar(missed_b[:, :], missed[:, 3:4], 1.0, None, ALU.min).then_inc(missed_ready, 1)
            dve.wait_ge(redo_psum, 1)
            nc.vector.tensor_copy(redo_i[:, :], ps_cnt[0:1, 2 * S2:2 * S2 + 1]).then_inc(redo_ready, 1)

            with dve.If(must_redo(dve)):
                st.did(nc.vector.tensor_copy(cols[:, 0, :], h_all[:, :, TCOL]))
                st.wait()
                nc.vector.tensor_copy(cols[:, 1, :], h_all[:, :, FCOL]).then_inc(cols_ready, 1)
                dve.wait_ge(rows_psum, 1)
                nc.vector.tensor_copy(rows[:, :, :], ps_misc[0:TILES, 0:2 * P].rearrange("c (r p) -> c r p", p=P)
                                      ).then_inc(rows_ready, 1)
                dve.wait_ge(rows_landed, 32)
                dve.sem_inc(d_free, 1)
                st.restart()
                with dve.Fori(0, TILES) as t:
                    def step(ins):
                        st.did(ins)
                        st.wait()

                    dve.wait_ge(d_adj_landed, 16 * (t + 1))
                    step(nc.vector.scalar_tensor_tensor(out=d_valid, in0=d_adj, scalar=0.0, in1=flag_row,
                                                        op0=ALU.is_gt, op1=ALU.mult))
                    step(nc.vector.reduce_sum(one[:, 0:1], d_valid, AX_X))
                    step(nc.vector.tensor_scalar(d_valid, d_valid, BIG, -BIG, ALU.mult, ALU.add))
                    step(nc.vector.tensor_tensor(d_att, d_valid, t_row, ALU.add))
                    step(nc.vector.reduce_max(one[:, 1:2], d_att, AX_X))
                    step(nc.vector.tensor_copy(one[:, 2:3], s_all[:, bass.ds(t, 1)]))
                    step(nc.vector.tensor_tensor(one[:, 3:4], one[:, 1:2], one[:, 2:3], ALU.add))
                    step(nc.vector.scalar_tensor_tensor(out=one[:, 1:2], in0=one[:, 3:4], scalar=ALPHA,
                                                        in1=one[:, 3:4], op0=ALU.mult, op1=ALU.max))
                    step(nc.vector.tensor_scalar(one[:, 3:4], one[:, 1:2], FLOOR, None, ALU.max))
                    step(nc.vector.tensor_scalar(one[:, 4:5], one[:, 3:4], -1.0, None, ALU.mult))
                    step(nc.vector.tensor_scalar(d_att, d_att, one[:, 2:3], None, ALU.add))
                    nc.vector.scalar_tensor_tensor(out=d_att, in0=d_att, scalar=ALPHA, in1=d_att,
                                                   op0=ALU.mult, op1=ALU.max).then_inc(d_score_ready, 1)
                    dve.wait_ge(d_prob_ready, t + 1)
                    step(nc.vector.tensor_scalar(one[:, 6:7], one[:, 5:6], 1.0 / BIG, None, ALU.max))
                    step(nc.vector.reciprocal(one[:, 7:8], one[:, 6:7]))
                    step(nc.vector.scalar_tensor_tensor(out=one[:, 8:9], in0=one[:, 7:8], scalar=THR, in1=one[:, 0:1],
                                                        op0=ALU.is_gt, op1=ALU.mult))
                    step(nc.vector.tensor_scalar(d_att, d_att, one[:, 7:8], None, ALU.mult))
                    nc.vector.scalar_tensor_tensor(out=d_att, in0=d_att, scalar=THR, in1=d_att,
                                                   op0=ALU.is_ge, op1=ALU.mult).then_inc(d_att_ready, 1)
                    with dve.Fori(0, GROUPS_D) as g:
                        dve.wait_ge(d_T_psum, GROUPS_D * t + g + 2)
                        nc.vector.tensor_copy(attT, ps_DT).then_inc(d_T_ready, 1)
                    dve.wait_ge(d_acc_psum, GROUPS_D * (t + 1))
                    step(nc.vector.scalar_tensor_tensor(
                        out=zacc[:, 0, :], in0=ps_acc, scalar=one[:, 8:9],
                        in1=h_all[:, bass.ds(t, 1), 0:D].rearrange("p a d -> p (a d)"), op0=ALU.mult, op1=ALU.add))
                    nc.vector.tensor_scalar(neg[:, 0, :], zacc[:, 0, :], 0.0, None, ALU.min).then_inc(d_neg_ready, 1)
                    dve.wait_ge(d_eneg_ready, t + 1)
                    step(nc.vector.scalar_tensor_tensor(out=rsum[:, 0, :], in0=zacc[:, 0, :], scalar=0.0,
                                                        in1=eneg[:, 0, :], op0=ALU.max, op1=ALU.add))
                    dve.wait_ge(d_x_landed, 16 * (t + 1))
                    nc.vector.scalar_tensor_tensor(out=ob[:, 0, 0, :], in0=rsum[:, 0, :], scalar=-1.0,
                                                   in1=xr[:, 0, 0, :], op0=ALU.add, op1=ALU.add
                                                   ).then_inc(d_out_ready, 1)
                    dve.wait_ge(d_stored, 16 * (t + 1))
                    dve.sem_inc(d_free, 1)
                    st.restart()


_INS = ["x", "adj", "L0_gnn_W", "L0_gnn_a"]


def kernel(**inputs):
    import numpy as _np
    import concourse.bacc as _bacc
    from concourse import mybir as _mybir
    from concourse.bass_utils import run_bass_kernel_spmd as _run

    nc = _bacc.Bacc("TRN2", target_bir_lowering=False, num_devices=1)
    arrays, args = {}, []
    for name in _INS:
        v = _np.ascontiguousarray(inputs[name])
        arrays[f"in_{name}_dram"] = v
        args.append(nc.dram_tensor(f"in_{name}_dram", v.shape, _mybir.dt.from_np(v.dtype), kind="ExternalInput").ap())
    n, d = inputs["x"].shape
    out = nc.dram_tensor("out_0_dram", (n, d), _mybir.dt.float32, kind="ExternalOutput").ap()
    table = nc.dram_tensor("table_dram", (n, d + 4), _mybir.dt.float32, kind="Internal").ap()
    trow = nc.dram_tensor("trow_dram", (2, n), _mybir.dt.float32, kind="Internal").ap()
    gat_kernel(nc, *args, out, table, trow)
    r = _run(nc, [arrays], core_ids=[0])
    return r.results[0]["out_0_dram"]
```

```python
from contextlib import ExitStack

import concourse.bass as bass
from concourse import mybir

F32 = mybir.dt.float32
BF16 = mybir.dt.bfloat16
I32 = mybir.dt.int32
ALU = mybir.AluOpType
ACT = mybir.ActivationFunctionType
AX_X = mybir.AxisListType.X

P = 128
EPS = 1e-5
THR = 1e-4
ALPHA = 0.2
BIG = 1e30
FLOOR = -1e29

BITS = 8
SEG = 128
SLOTS = 16
DIRECT = 6
RANKS = SLOTS - DIRECT
CHUNKS = 2
XPARTS = 4
UNIT = 4


class Steps:

    def __init__(self, eng, sem):
        self.eng, self.sem, self.n = eng, sem, 0

    def did(self, ins):
        self.n += 1
        ins.then_inc(self.sem, 1)

    def wait(self, back=0):
        self.eng.wait_ge(self.sem, self.n - back)

    def restart(self):
        self.wait()
        self.eng.sem_clear(self.sem)
        self.n = 0


def wait_alone(eng, sem, value, waits):
    eng.wait_ge(sem, value)
    eng.sem_inc(waits, 1)


def gat_kernel(nc, x, adj, W, a, out, table, trow):
    N, D = x.shape
    TILES = N // P
    PAIRS = TILES // 2
    GROUPS = N // BITS
    NSEG = GROUPS // SEG
    CW = N // CHUNKS
    TW = table.shape[1]
    TCOL, FCOL, SCOL = D, D + 1, D + 2
    PART = TILES // XPARTS
    UNITS = TILES // UNIT
    BIAS = float((2 ** BITS - 1) * GROUPS // 2)
    S2 = 2 * SLOTS
    WIN = P + RANKS
    NG = 2 * DIRECT + 1

    x_t = x.rearrange("(t p) d -> p t d", p=P)
    out_t = out.rearrange("(t p) d -> p t d", p=P)
    adj_t = adj.rearrange("(t p) j -> p t j", p=P)
    table_t = table.rearrange("(t p) d -> p t d", p=P)

    with ExitStack() as ctx:
        def sb(name, shape, dt):
            return ctx.enter_context(nc.sbuf_tensor(name, shape, dt))

        def ps(name, shape, dt):
            return ctx.enter_context(nc.psum_tensor(name, shape, dt))

        def sem(name):
            return ctx.enter_context(nc.semaphore(name))

        adj_sb = sb("adj_sb", [P, 2 * CHUNKS, CW], I32)
        mask = sb("mask", [P, 2 * CHUNKS, CW], BF16)
        x_all = sb("x_all", [P, TILES, D], F32)
        h_all = sb("h_all", [P, TILES, TW], F32)
        gath = x_all[:, :, :].rearrange("p t d -> p (t d)")[:, 0:2 * NG * TW].rearrange(
            "p (a s c) -> p a s c", a=2, c=TW)
        sq = sb("sq", [P, 2, PART, D], F32)

        d_adj = adj_sb[:, 0:CHUNKS, :].rearrange("p c w -> p (c w)")
        d_valid = d_adj.bitcast(F32)
        d_att = adj_sb[:, CHUNKS:2 * CHUNKS, :].rearrange("p c w -> p (c w)").bitcast(F32)
        t_row = mask[:, :, :].rearrange("p c w -> p (c w)").bitcast(F32)
        flag_row = x_all[:, :, :].rearrange("p t d -> p (t d)")
        missed = sb("missed", [P, 5], F32)
        redo_i = sb("redo_i", [1, 1], I32)
        cols = sb("cols", [P, 2, TILES], F32)
        rows = sb("rows", [TILES, 2, P], F32)
        one = sb("one", [P, 10], F32)

        ident = sb("ident", [P, P], F32)
        pack_w = sb("pack_w", [P, BITS, P], BF16)
        ones_b = sb("ones_b", [P, P], BF16)
        word_no = sb("word_no", [P, GROUPS], BF16)
        bit_mask = sb("bit_mask", [P, BITS], I32)
        bit_base = sb("bit_base", [P, BITS], I32)

        before = sb("before", [P, P], BF16)
        win_no = sb("win_no", [P, WIN], BF16)
        count = sb("count", [P, 2 * P], F32)
        row_rank = sb("row_rank", [P, 2, RANKS, 2], BF16)
        ones_f = sb("ones_f", [P, 1], F32)
        minus_half = sb("minus_half", [P, 1], F32)

        w_ext = sb("w_ext", [P, D + 3], F32)
        wT = sb("wT", [P, D], F32)
        a3 = sb("a3", [P, 3], F32)
        reluT = sb("reluT", [P, 2, UNIT, P], F32)
        s_all = sb("s_all", [P, TILES], F32)
        mean = sb("mean", [P, TILES], F32)
        var = sb("var", [P, TILES], F32)
        std = sb("std", [P, TILES], F32)
        rstd = sb("rstd", [P, TILES], F32)
        sum1 = sb("sum1", [P, TILES], F32)

        cand = sb("cand", [P, 2, NSEG * 8], F32)
        cand2 = sb("cand2", [P, 2, NSEG * 8], F32)
        words = sb("words", [P, S2], F32)
        words_i = sb("words_i", [P, S2], I32)
        word_n = sb("word_n", [P, S2], I32)
        bits = sb("bits", [P, S2, BITS], I32)
        keyf = sb("keyf", [P, S2, BITS], F32)
        ekey = sb("ekey", [P, S2, BITS], F32)
        ekey2 = sb("ekey2", [P, S2, BITS], F32)
        keys = sb("keys", [P, 2, S2], F32)
        idx = sb("idx", [P, 2, NG], I32)
        has = sb("has", [P, 2, SLOTS], BF16)
        extra = sb("extra", [P, 2], BF16)
        feat = sb("feat", [P, 2, RANKS, 4], BF16)
        place = sb("place", [P, 2, 2, WIN], BF16)
        entry = sb("entry", [P, 2, 4], F32)
        ekey1 = sb("ekey1", [P, 1], F32)
        used = sb("used", [P, 2], F32)
        found = sb("found", [P, 2, DIRECT], F32)
        found_l = sb("found_l", [P, 1], F32)
        sgn_sum = sb("sgn_sum", [P, TILES * CHUNKS], F32)

        t_flag = sb("t_flag", [P, 2], F32)
        owner = sb("owner", [P, 2 * P], F32)
        by_rank = sb("by_rank", [P, 2, RANKS], F32)
        valid = sb("valid", [P, S2], F32)
        t_s = sb("t_s", [P, S2], F32)
        w_rest = sb("w_rest", [P, 2, RANKS], F32)
        w_parts = sb("w_parts", [P, 2, RANKS, 3], BF16)
        w_entry = sb("w_entry", [P, 1], F32)
        scaled = sb("scaled", [P, D], F32)
        deg = sb("deg", [P, 2], F32)
        tm = sb("tm", [P, S2], F32)
        tm2 = sb("tm2", [P, S2], F32)
        mx = sb("mx", [P, 4, 2], F32)
        sc = sb("sc", [P, 3, S2], F32)
        prob = sb("prob", [P, S2], F32)
        zz = sb("zz", [P, 4, 2], F32)
        att = sb("att", [P, 3, S2], F32)
        zacc, zall, neg, eneg, rsum = [sq[:, 1, 2 * v:2 * v + 2, :] for v in range(5)]
        xr = sb("xr", [P, 2, 2, D], F32)
        ob = sb("ob", [P, 2, 2, D], F32)

        ps_words = [ps(f"ps_words{i}", [P, GROUPS], F32) for i in range(2)]
        ps_T = [ps(f"ps_T{i}", [P, UNIT, P], F32) for i in range(2)]
        ps_cnt = ps("ps_cnt", [P, 512], F32)
        ps_misc = ps("ps_misc", [P, 512], F32)
        ps_H = [ps_words[i][:, :].rearrange("p (t c) -> p t c", t=UNIT)[:, :, 0:D + 3] for i in range(2)]

        ps_first = ps_T[0][:, 0, 0:2]
        ps_entry = ps_T[1][:, 0, 0:4]
        ps_t = ps_cnt[:, 0:4 * RANKS].rearrange("p (t v r) -> p t v r", t=2, v=2)
        ps_sum = ps_misc[:, 0:2 * D].rearrange("p (t d) -> p t d", d=D)
        ps_w = ps_misc[:, 2 * D:2 * D + 3]

        const_ready = sem("const_ready")
        pool_steps = sem("pool_steps")
        pool_waits = sem("pool_waits")
        dve_steps = sem("dve_steps")
        dve_waits = sem("dve_waits")
        x_landed = [sem(f"x_landed{i}") for i in range(XPARTS)]
        w_landed = sem("w_landed")
        adj_landed = [sem(f"adj_landed{i}") for i in range(2 * CHUNKS)]
        xc_ready = sem("xc_ready")
        sq_ready = sem("sq_ready")
        var_ready = sem("var_ready")
        std_ready = sem("std_ready")
        wT_psum = sem("wT_psum")
        wT_ready = sem("wT_ready")
        we_psum = sem("we_psum")
        we_ready = sem("we_ready")
        reluT_psum = sem("reluT_psum")
        reluT_ready = sem("reluT_ready")
        h_psum = sem("h_psum")
        h_ready = sem("h_ready")
        part_ready = sem("part_ready")
        table_stored = sem("table_stored")
        mask_ready = sem("mask_ready")
        mask_used = sem("mask_used")
        words_ready = sem("words_ready")
        words_used = sem("words_used")
        idx_ready = sem("idx_ready")
        extra_ready = sem("extra_ready")
        first_psum = sem("first_psum")
        place_ready = sem("place_ready")
        entry_psum = sem("entry_psum")
        list_ready = sem("list_ready")
        by_rank_ready = sem("by_rank_ready")
        t_psum = sem("t_psum")
        w_ready = sem("w_ready")
        w_psum = sem("w_psum")
        scaled_ready = sem("scaled_ready")
        sum_psum = sem("sum_psum")
        gathered = [sem(f"gathered{i}") for i in range(2)]
        score_ready = sem("score_ready")
        prob_ready = sem("prob_ready")
        neg_ready = sem("neg_ready")
        eneg_ready = sem("eneg_ready")
        xr_landed = [sem(f"xr_landed{i}") for i in range(2)]
        out_ready = sem("out_ready")
        out_stored = [sem(f"out_stored{i}") for i in range(2)]

        missed_ready = sem("missed_ready")
        redo_psum = sem("redo_psum")
        redo_ready = sem("redo_ready")
        cols_ready = sem("cols_ready")
        rows_psum = sem("rows_psum")
        rows_ready = sem("rows_ready")
        rows_stored = sem("rows_stored")
        rows_landed = sem("rows_landed")
        d_free = sem("d_free")
        d_adj_landed = sem("d_adj_landed")
        d_x_landed = sem("d_x_landed")
        d_score_ready = sem("d_score_ready")
        d_prob_ready = sem("d_prob_ready")
        d_att_ready = sem("d_att_ready")
        d_stage_ready = sem("d_stage_ready")
        d_T_psum = sem("d_T_psum")
        d_T_ready = sem("d_T_ready")
        d_acc_psum = sem("d_acc_psum")
        d_neg_ready = sem("d_neg_ready")
        d_eneg_ready = sem("d_eneg_ready")
        d_out_ready = sem("d_out_ready")
        d_stored = sem("d_stored")
        GROUPS_D = TILES // UNIT
        stage, attT = sq[:, 0, 0:UNIT, :], reluT[:, 0, :, :]
        ps_DT = ps_T[0][:, :, :]
        ps_acc = ps_words[1][:, 0:D]

        def must_redo(eng):
            eng.wait_ge(redo_ready, 1)
            return eng.value_load(redo_i[0:1, 0:1], min_val=0, max_val=1) > 0

        block = ctx.enter_context(nc.Block())

        @block.sync
        def _(sp):
            def load_adj(i, par):
                q = 2 * i + par
                for b in range(2 * CHUNKS):
                    ti, c = b // CHUNKS, b % CHUNKS
                    if not (isinstance(q, int) and q == 0):
                        sp.wait_ge(mask_ready, 2 * CHUNKS * q + (b + 1 - 2 * CHUNKS))
                    sp.dma_start(adj_sb[:, b, :], adj_t[:, bass.ds(2 * q + ti, 1), c * CW:(c + 1) * CW]
                                 ).then_inc(adj_landed[b], 16)

            def load_x(i, par):
                q = 2 * i + par
                if not (isinstance(i, int) and i == 0):
                    sp.wait_ge(out_ready, q - 1)
                sp.dma_start(xr[:, par, :, :], x_t[:, bass.ds(2 * q, 2), :]).then_inc(xr_landed[par], 16)

            def store(i, par):
                q = 2 * i + par
                sp.wait_ge(out_ready, q + 1)
                sp.dma_start(out_t[:, bass.ds(2 * q, 2), :], ob[:, par, :, :]).then_inc(out_stored[par], 16)

            for k in range(XPARTS):
                sp.dma_start(x_all[:, k * PART:(k + 1) * PART, :], x_t[:, k * PART:(k + 1) * PART, :]
                             ).then_inc(x_landed[k], 16)
                if k == 0:
                    sp.dma_start(w_ext[:, 0:D], W).then_inc(w_landed, 16)
                    sp.dma_start(a3[:, 0:1], a[D:2 * D, :]).then_inc(w_landed, 16)
                    sp.dma_start(a3[:, 2:3], a[0:D, :]).then_inc(w_landed, 16)
            load_adj(0, 0)
            load_adj(0, 1)
            for par in range(2):
                load_adj(1, par)
                load_x(0, par)
            with sp.Fori(2, PAIRS // 2) as i:
                for par in range(2):
                    load_adj(i, par)
                    load_x(i - 1, par)
                    store(i - 2, par)
            for par in range(2):
                load_x(PAIRS // 2 - 1, par)
                store(PAIRS // 2 - 2, par)
            for par in range(2):
                store(PAIRS // 2 - 1, par)
            for par in range(2):
                sp.wait_ge(out_stored[par], 16 * (PAIRS // 2))

            with sp.If(must_redo(sp)):
                sp.wait_ge(rows_ready, 1)
                for r in range(2):
                    sp.dma_start(trow[r:r + 1, :].rearrange("a (c p) -> (a c) p", p=P), rows[:, r, :]
                                 ).then_inc(rows_stored, 16)
                sp.wait_ge(rows_stored, 32)
                sp.dma_start(t_row, trow[0:1, :].to_broadcast([P, N])).then_inc(rows_landed, 16)
                sp.dma_start(flag_row, trow[1:2, :].to_broadcast([P, N])).then_inc(rows_landed, 16)
                with sp.Fori(0, TILES) as t:
                    sp.wait_ge(d_free, t + 1)
                    sp.dma_start(d_adj, adj_t[:, bass.ds(t, 1), :].rearrange("p a j -> p (a j)")
                                 ).then_inc(d_adj_landed, 16)
                    sp.dma_start(xr[:, 0, 0:1, :], x_t[:, bass.ds(t, 1), :]).then_inc(d_x_landed, 16)
                    sp.wait_ge(d_out_ready, t + 1)
                    sp.dma_start(out_t[:, bass.ds(t, 1), :], ob[:, 0, 0:1, :]).then_inc(d_stored, 16)
                sp.wait_ge(d_stored, 16 * TILES)

        @block.gpsimd
        def _(pool):
            st = Steps(pool, pool_steps)

            def made(ins):
                st.did(ins)
                st.wait()

            made(nc.gpsimd.memset(a3[:, 1:2], 1.0))
            made(nc.gpsimd.memset(ident[:, :], 0.0))
            made(nc.gpsimd.affine_select(out=ident[:, :], in_=ident[:, :], compare_op=ALU.not_equal, fill=1.0,
                                         base=0, pattern=[[-1, P]], channel_multiplier=1))
            made(nc.gpsimd.memset(minus_half[:, :], -0.5))
            pool.sem_inc(const_ready, 1)
            made(nc.gpsimd.memset(pack_w[:, :, :], 0.0))
            for b in range(BITS):
                made(nc.gpsimd.affine_select(out=pack_w[:, b, :], in_=pack_w[:, b, :], compare_op=ALU.not_equal,
                                             fill=float(2 ** b * GROUPS // 2), base=0, pattern=[[-1, P]],
                                             channel_multiplier=1))
            made(nc.gpsimd.memset(ones_b[:, :], 1.0))
            made(nc.gpsimd.memset(word_no[:, :], 0.0))
            hi = GROUPS // P
            made(nc.gpsimd.iota(word_no[0:1, :].rearrange("p (h l) -> p h l", l=P), [[-P, hi], [0, P]],
                                base=GROUPS - P, channel_multiplier=0, allow_small_or_imprecise_dtypes=True))
            made(nc.gpsimd.iota(word_no[32:33, :].rearrange("p (h l) -> p h l", l=P), [[0, hi], [-1, P]],
                                base=P - 1, channel_multiplier=0, allow_small_or_imprecise_dtypes=True))
            for b in range(BITS):
                made(nc.gpsimd.memset(bit_mask[:, b:b + 1], GROUPS * 2 ** b))
            made(nc.gpsimd.iota(bit_base[:, :], [[-GROUPS, BITS]], base=1 + GROUPS * (BITS - 1),
                                channel_multiplier=0))
            made(nc.gpsimd.memset(before[:, :], 1.0))
            made(nc.gpsimd.affine_select(out=before[:, :], in_=before[:, :], compare_op=ALU.is_gt, fill=0.0,
                                         base=0, pattern=[[1, P]], channel_multiplier=-1))
            made(nc.gpsimd.iota(win_no[:, :], [[1, WIN]], base=-RANKS, channel_multiplier=0,
                                allow_small_or_imprecise_dtypes=True))
            made(nc.gpsimd.iota(count[:, :], [[1, 2 * P]], base=0, channel_multiplier=0,
                                allow_small_or_imprecise_dtypes=True))
            made(nc.gpsimd.iota(row_rank[:, :, :, 0], [[P, 2], [0, RANKS]], base=0, channel_multiplier=1,
                                allow_small_or_imprecise_dtypes=True))
            made(nc.gpsimd.iota(row_rank[:, :, :, 1], [[0, 2], [1, RANKS]], base=0, channel_multiplier=0,
                                allow_small_or_imprecise_dtypes=True))
            made(nc.gpsimd.memset(ones_f[:, :], 1.0))
            made(nc.gpsimd.memset(h_all[:, :, SCOL + 1:TW], 0.0))
            pool.sem_inc(const_ready, 1)

            def gather(par, s):
                nc.gpsimd.indirect_dma_start(
                    gath[:, par, s, :], None, table[:, :],
                    bass.IndirectOffsetOnAxis(ap=idx[:, par, s:s + 1], axis=0),
                    bounds_check=N - 1, oob_is_err=False).then_inc(gathered[par], 16)

            def pair(i, par):
                q = 2 * i + par
                if not (isinstance(i, int) and i == 0):
                    pool.wait_ge(scaled_ready, q - 1)
                wait_alone(pool, idx_ready, q + 1, pool_waits)
                for s in range(2 * DIRECT):
                    gather(par, s)
                wait_alone(pool, list_ready, q + 1, pool_waits)
                gather(par, 2 * DIRECT)

            for k in range(XPARTS):
                pool.wait_ge(part_ready, k + 1)
                pool.dma_start(table_t[:, k * PART:(k + 1) * PART, :], h_all[:, k * PART:(k + 1) * PART, :]
                               ).then_inc(table_stored, 16)
            pool.wait_ge(table_stored, 16 * XPARTS)
            pair(0, 0)
            pair(0, 1)
            with pool.Fori(1, PAIRS // 2) as i:
                pair(i, 0)
                pair(i, 1)

        @block.scalar
        def _(act):
            def square(k):
                act.wait_ge(xc_ready, k + 1)
                if k >= 2:
                    act.wait_ge(var_ready, k - 1)
                nc.scalar.activation(sq[:, k % 2, :, :], x_all[:, k * PART:(k + 1) * PART, :],
                                     ACT.Square).then_inc(sq_ready, 1)

            def root(k):
                part = slice(k * PART, (k + 1) * PART)
                act.wait_ge(var_ready, k + 1)
                nc.scalar.activation(std[:, part], var[:, part], ACT.Sqrt).then_inc(std_ready, 1)

            def relu(units):
                for u in units:
                    act.wait_ge(reluT_psum, u + 1)
                    if u >= 2:
                        act.wait_ge(h_psum, u - 1)
                    nc.scalar.activation(reluT[:, u % 2, :, :], ps_T[u % 2][:, :, :],
                                         ACT.Relu).then_inc(reluT_ready, 1)

            def cast(i, par, b):
                q = 2 * i + par
                act.wait_ge(adj_landed[b], 16 * (q + 1))
                if not (isinstance(q, int) and q == 0):
                    act.wait_ge(mask_used, 2 * CHUNKS * q + (b + 1 - 2 * CHUNKS))
                nc.scalar.activation(mask[:, b, :], adj_sb[:, b, :], ACT.Sign, bias=minus_half[:, 0:1],
                                     accum_out=sgn_sum[:, bass.ds(2 * CHUNKS * q + b, 1)]
                                     ).then_inc(mask_ready, 1)

            def exp_scores(q):
                act.wait_ge(score_ready, q + 1)
                nc.scalar.activation(prob[:, :], sc[:, 2, :], ACT.Exp).then_inc(prob_ready, 1)

            def exp_neg(q):
                act.wait_ge(neg_ready, q + 1)
                nc.scalar.activation(eneg[:, :, :], neg[:, :, :], ACT.Exp).then_inc(eneg_ready, 1)

            def pair(i, par, lag):
                q = 2 * i + par
                cast(i, par, 0)
                if lag >= 3:
                    exp_neg(q - 3)
                cast(i, par, 1)
                cast(i, par, 2)
                if lag >= 2:
                    exp_scores(q - 2)
                cast(i, par, 3)

            square(0)
            relu(range(0, 2))
            square(1)
            root(0)
            relu(range(2, 4))
            square(2)
            root(1)
            relu(range(4, 7))
            act.wait_ge(const_ready, 1)
            cast(0, 0, 0)
            square(3)
            root(2)
            relu(range(7, 9))
            cast(0, 0, 1)
            root(3)
            relu(range(9, 11))
            cast(0, 0, 2)
            relu(range(11, 13))
            cast(0, 0, 3)
            relu(range(13, UNITS))
            pair(0, 1, 1)
            pair(1, 0, 2)
            pair(1, 1, 3)
            with act.Fori(2, PAIRS // 2) as i:
                pair(i, 0, 3)
                pair(i, 1, 3)
            exp_neg(PAIRS - 3)
            exp_scores(PAIRS - 2)
            exp_neg(PAIRS - 2)
            exp_scores(PAIRS - 1)
            exp_neg(PAIRS - 1)

            with act.If(must_redo(act)):
                with act.Fori(0, TILES) as t:
                    act.wait_ge(d_score_ready, t + 1)
                    nc.scalar.activation(d_att, d_att, ACT.Exp, bias=one[:, 4:5], accum_out=one[:, 5:6]
                                         ).then_inc(d_prob_ready, 1)
                    act.wait_ge(d_att_ready, t + 1)
                    with act.Fori(0, GROUPS_D) as g:
                        act.wait_ge(d_T_psum, GROUPS_D * t + g + 1)
                        nc.scalar.copy(stage.rearrange("p t d -> p (t d)"), d_att[:, bass.ds(UNIT * P * g, UNIT * P)]
                                       ).then_inc(d_stage_ready, 1)
                    act.wait_ge(d_neg_ready, t + 1)
                    nc.scalar.activation(eneg[:, 0, :], neg[:, 0, :], ACT.Exp).then_inc(d_eneg_ready, 1)

        @block.tensor
        def _(pe):
            pe.wait_ge(const_ready, 1)
            pe.wait_ge(w_landed, 48)
            nc.tensor.transpose(ps_misc[:, 0:D], w_ext[:, 0:D], ident[:, :]).then_inc(wT_psum, 1)
            pe.wait_ge(wT_ready, 1)
            nc.tensor.matmul(ps_misc[:, D:D + 3], wT[:, :], a3[:, :], start=True, stop=True).then_inc(we_psum, 1)
            pe.wait_ge(we_ready, 1)

            def transposes(u):
                pe.wait_ge(xc_ready, u // (UNITS // XPARTS) + 1)
                if u >= 2:
                    pe.wait_ge(reluT_ready, u - 1)
                for t in range(UNIT):
                    last = nc.tensor.transpose(ps_T[u % 2][:, t, :], x_all[:, UNIT * u + t, :], ident[:, :])
                last.then_inc(reluT_psum, 1)

            def project(u):
                pe.wait_ge(reluT_ready, u + 1)
                if u >= 2:
                    pe.wait_ge(h_ready, u - 1)
                for t in range(UNIT):
                    last = nc.tensor.matmul(ps_H[u % 2][:, t, :], reluT[:, u % 2, t, :], w_ext[:, :],
                                            start=True, stop=True)
                last.then_inc(h_psum, 1)

            transposes(0)
            for u in range(1, UNITS):
                transposes(u)
                project(u - 1)
            project(UNITS - 1)
            pe.wait_ge(h_ready, UNITS)
            pe.wait_ge(const_ready, 2)

            def pack(i, par, b):
                q, ti, c = 2 * i + par, b // CHUNKS, b % CHUNKS
                per = BITS // CHUNKS
                if c == 0 and not (isinstance(q, int) and q == 0):
                    pe.wait_ge(words_used, 2 * q + ti - 1)
                pe.wait_ge(mask_ready, 2 * CHUNKS * q + b + 1)
                for bit in range(per):
                    for bank in range(GROUPS // 512):
                        last = nc.tensor.matmul(
                            ps_words[ti][:, bank * 512:(bank + 1) * 512], pack_w[:, c * per + bit, :],
                            mask[:, b, bit * GROUPS + bank * 512:bit * GROUPS + (bank + 1) * 512],
                            start=(c == 0 and bit == 0), stop=False)
                last.then_inc(mask_used, 1)
                if c == CHUNKS - 1:
                    for bank in range(GROUPS // 512):
                        last = nc.tensor.matmul(ps_words[ti][:, bank * 512:(bank + 1) * 512], ones_b[:, :],
                                                word_no[:, bank * 512:(bank + 1) * 512], start=False, stop=True)
                    last.then_inc(words_ready, 1)

            def windows(par):
                for ti in range(2):
                    for r in range(RANKS):
                        yield ti, r, place[:, par, ti, RANKS - r:RANKS - r + P]

            def make_list(q, par):
                pe.wait_ge(extra_ready, q + 1)
                nc.tensor.matmul(ps_first, before[:, :], extra[:, :], start=True, stop=False)
                nc.tensor.matmul(ps_first[:, 1:2], ones_b[:, :], extra[:, 0:1], start=False, stop=True
                                 ).then_inc(first_psum, 1)
                pe.wait_ge(place_ready, q + 1)
                for ti, r, window in windows(par):
                    last = nc.tensor.matmul(ps_entry, window, feat[:, ti, r, :], start=(ti == 0 and r == 0),
                                            stop=(ti == 1 and r == RANKS - 1))
                last.then_inc(entry_psum, 1)

            def list_scores(q):
                pe.wait_ge(by_rank_ready, q + 1)
                for ti in range(2):
                    last = nc.tensor.matmul(ps_t[:, ti, :, :].rearrange("p v r -> p (v r)"),
                                            owner[:, ti * P:(ti + 1) * P],
                                            by_rank[:, :, :].rearrange("p v r -> p (v r)"), start=True, stop=True)
                last.then_inc(t_psum, 1)

            def list_weights(q, par):
                pe.wait_ge(w_ready, q + 1)
                for ti, r, window in windows(par):
                    last = nc.tensor.matmul(ps_w, window, w_parts[:, ti, r, :], start=(ti == 0 and r == 0),
                                            stop=(ti == 1 and r == RANKS - 1))
                last.then_inc(w_psum, 1)

            def list_sum(q):
                pe.wait_ge(scaled_ready, q + 1)
                for ti in range(2):
                    last = nc.tensor.matmul(ps_sum[:, ti, :], owner[:, ti * P:(ti + 1) * P], scaled[:, :],
                                            start=True, stop=True)
                last.then_inc(sum_psum, 1)

            def pair(i, par, lag):
                q = 2 * i + par
                pack(i, par, 0)
                if lag >= 1:
                    make_list(q - 1, 1 - par)
                pack(i, par, 1)
                if lag >= 2:
                    list_scores(q - 2)
                pack(i, par, 2)
                if lag >= 2:
                    list_weights(q - 2, par)
                pack(i, par, 3)
                if lag >= 2:
                    list_sum(q - 2)

            pair(0, 0, 0)
            pair(0, 1, 1)
            with pe.Fori(1, PAIRS // 2) as i:
                pair(i, 0, 2)
                pair(i, 1, 2)
            make_list(PAIRS - 1, 1)
            for par in range(2):
                list_scores(PAIRS - 2 + par)
                list_weights(PAIRS - 2 + par, par)
                list_sum(PAIRS - 2 + par)

            pe.wait_ge(missed_ready, 1)
            nc.tensor.matmul(ps_cnt[0:1, 4 * RANKS:4 * RANKS + 1], ones_f[:, :], missed[:, 3:4], start=True, stop=True
                             ).then_inc(redo_psum, 1)
            with pe.If(must_redo(pe)):
                pe.wait_ge(cols_ready, 1)
                for r in range(2):
                    last = nc.tensor.transpose(ps_misc[0:TILES, r * P:(r + 1) * P], cols[:, r, :], ident[:, :])
                last.then_inc(rows_psum, 1)
                pe.sem_inc(d_T_psum, 1)

                def group(t, g, start, stop):
                    pe.wait_ge(d_stage_ready, GROUPS_D * t + g + 1)
                    for k in range(UNIT):
                        last = nc.tensor.transpose(ps_DT[:, k, :], stage[:, k, :], ident[:, :])
                    last.then_inc(d_T_psum, 1)
                    pe.wait_ge(d_T_ready, GROUPS_D * t + g + 1)
                    for k in range(UNIT):
                        last = nc.tensor.matmul(
                            ps_acc, attT[:, k, :], h_all[:, bass.ds(UNIT * g + k, 1), 0:D].rearrange("p a d -> p (a d)"),
                            start=start and k == 0, stop=stop and k == UNIT - 1)
                    last.then_inc(d_acc_psum, 1)

                with pe.Fori(0, TILES) as t:
                    group(t, 0, True, False)
                    with pe.Fori(1, GROUPS_D - 1) as g:
                        group(t, g, False, False)
                    group(t, GROUPS_D - 1, False, True)

        @block.vector
        def _(dve):
            st = Steps(dve, dve_steps)
            dve.wait_ge(wT_psum, 1)
            nc.vector.tensor_copy(wT[:, :], ps_misc[:, 0:D]).then_inc(wT_ready, 1)
            dve.wait_ge(we_psum, 1)
            nc.vector.tensor_copy(w_ext[:, D:D + 3], ps_misc[:, D:D + 3]).then_inc(we_ready, 1)

            def centre(k):
                part = slice(k * PART, (k + 1) * PART)
                dve.wait_ge(x_landed[k], 16)
                st.did(nc.vector.reduce_sum(sum1[:, part], x_all[:, part, :], AX_X))
                st.wait()
                st.did(nc.vector.tensor_scalar(mean[:, part], sum1[:, part], 1.0 / D, None, ALU.mult))
                st.wait()
                nc.vector.tensor_tensor(x_all[:, part, :], x_all[:, part, :],
                                        mean[:, part].unsqueeze(2).to_broadcast([P, PART, D]),
                                        ALU.subtract).then_inc(xc_ready, 1)

            def variance(k):
                part = slice(k * PART, (k + 1) * PART)
                dve.wait_ge(sq_ready, k + 1)
                st.did(nc.vector.reduce_sum(sum1[:, part], sq[:, k % 2, :, :], AX_X))
                st.wait()
                nc.vector.tensor_scalar(var[:, part], sum1[:, part], 1.0 / D, EPS, ALU.mult, ALU.add
                                        ).then_inc(var_ready, 1)

            def scale(units):
                for u in units:
                    per = UNITS // XPARTS
                    k, part = u // per, slice(u // per * PART, (u // per + 1) * PART)
                    if u % per == 0:
                        dve.wait_ge(std_ready, k + 1)
                        st.did(nc.vector.reciprocal(rstd[:, part], std[:, part]))
                        st.wait()
                    tiles = slice(UNIT * u, UNIT * (u + 1))
                    dve.wait_ge(h_psum, u + 1)
                    nc.vector.tensor_tensor(h_all[:, tiles, 0:D + 3], ps_H[u % 2],
                                            rstd[:, tiles].unsqueeze(2).to_broadcast([P, UNIT, D + 3]),
                                            ALU.mult).then_inc(h_ready, 1)
                    if u % per == per - 1:
                        dve.wait_ge(h_ready, u + 1)
                        st.did(nc.vector.tensor_copy(s_all[:, part], h_all[:, part, SCOL]))
                        nc.vector.tensor_scalar(h_all[:, part, FCOL], h_all[:, part, FCOL], 0.0, None,
                                                ALU.not_equal).then_inc(part_ready, 1)

            centre(0)
            centre(1)
            variance(0)
            scale(range(0, 2))
            centre(2)
            variance(1)
            scale(range(2, 5))
            centre(3)
            variance(2)
            scale(range(5, 9))
            variance(3)
            scale(range(9, UNITS))
            st.did(nc.vector.memset(found[:, :, :], 0.0))
            st.did(nc.vector.memset(found_l[:, :], 0.0))
            dve.wait_ge(const_ready, 2)

            def per_tile(v):
                return v.unsqueeze(2).to_broadcast([P, 2, SLOTS])

            def by_tile(v):
                return v.rearrange("p (t k) -> p t k", k=SLOTS)

            def top16(out, rest, src, empty):
                st.did(nc.vector.max(out[:, 0:8], src))
                st.wait()
                st.did(nc.vector.match_replace(rest, out[:, 0:8], src, empty))
                st.wait()
                return nc.vector.max(out[:, 8:16], rest)

            def search(i, par, ti):
                wait_alone(dve, words_ready, 2 * (2 * i + par) + ti + 1, dve_waits)
                for s in range(NSEG):
                    st.did(nc.vector.max(cand[:, ti, s * 8:(s + 1) * 8],
                                         ps_words[ti][:, s * SEG:(s + 1) * SEG]))
                st.wait()
                dve.sem_inc(words_used, 1)
                st.did(top16(words[:, ti * SLOTS:(ti + 1) * SLOTS], cand2[:, ti, :], cand[:, ti, :], -BIG))

            def extract(i, par):
                q = 2 * i + par
                st.wait()
                st.did(nc.vector.tensor_scalar(words_i[:, :], words[:, :], BIAS, None, ALU.add))
                st.wait()
                st.did(nc.vector.tensor_scalar(word_n[:, :], words_i[:, :], GROUPS - 1, None, ALU.bitwise_and))
                st.did(nc.vector.tensor_tensor(bits[:, :, :], words_i[:, :].unsqueeze(2).to_broadcast([P, S2, BITS]),
                                               bit_mask[:, :].unsqueeze(1).to_broadcast([P, S2, BITS]),
                                               ALU.bitwise_and))
                st.wait(1)
                st.did(nc.vector.tensor_tensor(keyf[:, :, :], word_n[:, :].unsqueeze(2).to_broadcast([P, S2, BITS]),
                                               bit_base[:, :].unsqueeze(1).to_broadcast([P, S2, BITS]), ALU.add))
                st.wait()
                st.did(nc.vector.scalar_tensor_tensor(out=ekey[:, :, :], in0=bits[:, :, :], scalar=0.0,
                                                      in1=keyf[:, :, :], op0=ALU.is_gt, op1=ALU.mult))
                st.wait()
                for ti in range(2):
                    part = slice(ti * SLOTS, (ti + 1) * SLOTS)
                    st.did(top16(keys[:, par, part], ekey2[:, part, :].rearrange("p s b -> p (s b)"),
                                 ekey[:, part, :].rearrange("p s b -> p (s b)"), 0.0))
                st.wait()
                key = by_tile(keys[:, par, :])
                late = key[:, :, DIRECT:SLOTS]
                nc.vector.tensor_scalar(idx[:, par, 0:2 * DIRECT].rearrange("p (t k) -> p t k", k=DIRECT),
                                        key[:, :, 0:DIRECT], -1.0, float(N), ALU.mult, ALU.add).then_inc(idx_ready, 1)
                st.did(nc.vector.tensor_scalar(has[:, :, :], key, 0.0, None, ALU.is_gt))
                st.wait()
                with nc.allow_low_precision(reason="counts up to RANKS are exact in bfloat16"):
                    nc.vector.reduce_sum(extra[:, :], has[:, :, DIRECT:SLOTS], AX_X).then_inc(extra_ready, 1)
                st.did(nc.vector.tensor_copy(feat[:, :, :, 0], late))
                st.did(nc.vector.tensor_tensor(feat[:, :, :, 2:4],
                                               has[:, :, DIRECT:SLOTS].unsqueeze(3).to_broadcast([P, 2, RANKS, 2]),
                                               row_rank[:, :, :, :], ALU.mult))
                st.wait(1)
                st.did(nc.vector.tensor_tensor(feat[:, :, :, 1], late, feat[:, :, :, 0], ALU.subtract))
                st.did(nc.vector.tensor_tensor(found[:, :, :], found[:, :, :], has[:, :, 0:DIRECT], ALU.add))
                dve.wait_ge(first_psum, q + 1)
                st.wait()
                for ti in range(2):
                    last = nc.vector.tensor_scalar(place[:, par, ti, :], win_no[:, :], ps_first[:, ti:ti + 1], None,
                                                   ALU.is_equal)
                last.then_inc(place_ready, 1)
                dve.wait_ge(entry_psum, q + 1)
                st.did(nc.vector.tensor_copy(entry[:, par, :], ps_entry))
                st.wait()
                st.did(nc.vector.tensor_tensor(ekey1[:, :], entry[:, par, 0:1], entry[:, par, 1:2], ALU.add))
                st.wait()
                nc.vector.tensor_scalar(idx[:, par, 2 * DIRECT:NG], ekey1[:, :], -1.0, float(N), ALU.mult, ALU.add
                                        ).then_inc(list_ready, 1)
                st.did(nc.vector.tensor_scalar(used[:, par:par + 1], ekey1[:, :], 0.0, None, ALU.is_gt))
                st.wait()
                st.did(nc.vector.tensor_tensor(found_l[:, :], found_l[:, :], used[:, par:par + 1], ALU.add))

            def spread(i, par):
                q = 2 * i + par
                dve.wait_ge(gathered[par], 16 * NG * (i + 1))
                st.did(nc.vector.tensor_scalar(t_flag[:, :], gath[:, par, 2 * DIRECT, TCOL:FCOL + 1],
                                               used[:, par:par + 1], None, ALU.mult))
                st.did(nc.vector.tensor_scalar(owner[:, :], count[:, :], entry[:, par, 2:3], None, ALU.is_equal))
                st.wait(1)
                for v in range(2):
                    last = nc.vector.tensor_scalar(by_rank[:, v, :], count[:, 0:RANKS], entry[:, par, 3:4],
                                                   t_flag[:, v:v + 1], ALU.is_equal, ALU.mult)
                st.wait()
                last.then_inc(by_rank_ready, 1)

            def scores(i, par):
                q = 2 * i + par
                s_q = s_all[:, bass.ds(2 * q, 2)]
                slots = gath[:, par, 0:2 * DIRECT, :].rearrange("p (t k) c -> p t k c", k=DIRECT)
                st.did(nc.vector.scalar_tensor_tensor(
                    out=by_tile(valid[:, :])[:, :, 0:DIRECT], in0=by_tile(keys[:, par, :])[:, :, 0:DIRECT], scalar=0.0,
                    in1=slots[:, :, :, FCOL], op0=ALU.is_gt, op1=ALU.mult))
                st.did(nc.vector.tensor_copy(by_tile(t_s[:, :])[:, :, 0:DIRECT], slots[:, :, :, TCOL]))
                dve.wait_ge(t_psum, q + 1)
                st.did(nc.vector.tensor_copy(by_tile(t_s[:, :])[:, :, DIRECT:SLOTS], ps_t[:, :, 0, :]))
                st.did(nc.vector.tensor_copy(by_tile(valid[:, :])[:, :, DIRECT:SLOTS], ps_t[:, :, 1, :]))
                st.wait()
                st.did(nc.vector.tensor_scalar(tm[:, :], valid[:, :], BIG, -BIG, ALU.mult, ALU.add))
                st.did(nc.vector.reduce_sum(deg[:, :], by_tile(valid[:, :]), AX_X))
                st.wait(1)
                st.did(nc.vector.tensor_tensor(tm2[:, :], tm[:, :], t_s[:, :], ALU.add))
                st.wait()
                st.did(nc.vector.reduce_max(mx[:, 0, :], by_tile(tm2[:, :]), AX_X))
                st.did(nc.vector.tensor_tensor(by_tile(sc[:, 0, :]), by_tile(tm2[:, :]), per_tile(s_q), ALU.add))
                st.wait(1)
                st.did(nc.vector.tensor_tensor(mx[:, 1, :], mx[:, 0, :], s_q, ALU.add))
                st.wait(1)
                st.did(nc.vector.scalar_tensor_tensor(out=sc[:, 1, :], in0=sc[:, 0, :], scalar=ALPHA,
                                                      in1=sc[:, 0, :], op0=ALU.mult, op1=ALU.max))
                st.wait(1)
                st.did(nc.vector.scalar_tensor_tensor(out=mx[:, 2, :], in0=mx[:, 1, :], scalar=ALPHA,
                                                      in1=mx[:, 1, :], op0=ALU.mult, op1=ALU.max))
                st.wait()
                st.did(nc.vector.tensor_scalar(mx[:, 3, :], mx[:, 2, :], FLOOR, None, ALU.max))
                st.wait()
                nc.vector.tensor_tensor(by_tile(sc[:, 2, :]), by_tile(sc[:, 1, :]), per_tile(mx[:, 3, :]),
                                        ALU.subtract).then_inc(score_ready, 1)

            def aggregate(i, par):
                q = 2 * i + par
                dve.wait_ge(prob_ready, q + 1)
                st.did(nc.vector.reduce_sum(zz[:, 0, :], by_tile(prob[:, :]), AX_X))
                st.wait()
                st.did(nc.vector.tensor_scalar(zz[:, 1, :], zz[:, 0, :], 1.0 / BIG, None, ALU.max))
                st.wait()
                st.did(nc.vector.reciprocal(zz[:, 2, :], zz[:, 1, :]))
                st.wait()
                st.did(nc.vector.scalar_tensor_tensor(out=zz[:, 3, :], in0=zz[:, 2, :], scalar=THR, in1=deg[:, :],
                                                      op0=ALU.is_gt, op1=ALU.mult))
                st.did(nc.vector.tensor_tensor(by_tile(att[:, 0, :]), by_tile(prob[:, :]), per_tile(zz[:, 2, :]),
                                               ALU.mult))
                st.wait()
                st.did(nc.vector.scalar_tensor_tensor(out=att[:, 1, :], in0=att[:, 0, :], scalar=THR,
                                                      in1=att[:, 0, :], op0=ALU.is_ge, op1=ALU.mult))
                st.wait()
                st.did(nc.vector.tensor_tensor(by_tile(att[:, 2, :]), by_tile(att[:, 1, :]), per_tile(zz[:, 3, :]),
                                               ALU.mult))
                st.wait()
                late = by_tile(att[:, 2, :])[:, :, DIRECT:SLOTS]
                st.did(nc.vector.tensor_copy(w_parts[:, :, :, 0], late))
                st.wait()
                st.did(nc.vector.tensor_tensor(w_rest[:, :, :], late, w_parts[:, :, :, 0], ALU.subtract))
                st.wait()
                st.did(nc.vector.tensor_copy(w_parts[:, :, :, 1], w_rest[:, :, :]))
                st.wait()
                nc.vector.tensor_tensor(w_parts[:, :, :, 2], w_rest[:, :, :], w_parts[:, :, :, 1], ALU.subtract
                                        ).then_inc(w_ready, 1)
                for k in range(DIRECT):
                    for ti in range(2):
                        if k == 0:
                            so_far = h_all[:, bass.ds(2 * q + ti, 1), 0:D].rearrange("p a d -> p (a d)")
                        else:
                            so_far = zacc[:, ti, :]
                            st.wait(1)
                        st.did(nc.vector.scalar_tensor_tensor(
                            out=zacc[:, ti, :], in0=gath[:, par, ti * DIRECT + k, 0:D],
                            scalar=att[:, 2, ti * SLOTS + k:ti * SLOTS + k + 1],
                            in1=so_far, op0=ALU.mult, op1=ALU.add))
                dve.wait_ge(w_psum, q + 1)
                st.did(nc.vector.reduce_sum(w_entry[:, :], ps_w, AX_X))
                st.wait()
                nc.vector.tensor_scalar(scaled[:, :], gath[:, par, 2 * DIRECT, 0:D], w_entry[:, :], None, ALU.mult
                                        ).then_inc(scaled_ready, 1)

            def add_list(i, par):
                q = 2 * i + par
                dve.wait_ge(sum_psum, q + 1)
                st.did(nc.vector.tensor_tensor(zall[:, :, :], zacc[:, :, :], ps_sum, ALU.add))
                st.wait()
                nc.vector.tensor_scalar(neg[:, :, :], zall[:, :, :], 0.0, None, ALU.min).then_inc(neg_ready, 1)

            def finish(i, par):
                q = 2 * i + par
                dve.wait_ge(eneg_ready, q + 1)
                st.did(nc.vector.scalar_tensor_tensor(out=rsum[:, :, :], in0=zall[:, :, :], scalar=0.0,
                                                      in1=eneg[:, :, :], op0=ALU.max, op1=ALU.add))
                dve.wait_ge(xr_landed[par], 16 * (i + 1))
                if not (isinstance(i, int) and i == 0):
                    dve.wait_ge(out_stored[par], 16 * i)
                st.wait()
                nc.vector.scalar_tensor_tensor(out=ob[:, par, :, :], in0=rsum[:, :, :], scalar=-1.0,
                                               in1=xr[:, par, :, :], op0=ALU.add, op1=ALU.add
                                               ).then_inc(out_ready, 1)

            def pair(i, par, lag):
                if lag >= 1:
                    extract(i - 1 + par, 1 - par)
                if lag >= 3:
                    finish(i - 2 + par, 1 - par)
                if lag >= 2:
                    spread(i - 1, par)
                search(i, par, 0)
                if lag >= 2:
                    scores(i - 1, par)
                    aggregate(i - 1, par)
                search(i, par, 1)
                if lag >= 2:
                    add_list(i - 1, par)

            pair(0, 0, 0)
            pair(0, 1, 1)
            pair(1, 0, 2)
            pair(1, 1, 3)
            st.restart()
            with dve.Fori(2, PAIRS // 2) as i:
                pair(i, 0, 3)
                pair(i, 1, 3)
                st.restart()
            extract(PAIRS // 2 - 1, 1)
            finish(PAIRS // 2 - 2, 1)
            for par in range(2):
                spread(PAIRS // 2 - 1, par)
                scores(PAIRS // 2 - 1, par)
                aggregate(PAIRS // 2 - 1, par)
                add_list(PAIRS // 2 - 1, par)
                finish(PAIRS // 2 - 1, par)
            st.restart()

            dve.wait_ge(mask_ready, 2 * CHUNKS * PAIRS)
            st.did(nc.vector.reduce_sum(missed[:, 0:1], sgn_sum[:, :], AX_X))
            st.did(nc.vector.reduce_sum(missed[:, 1:2], found[:, :, :], mybir.AxisListType.XY))
            st.wait()
            st.did(nc.vector.tensor_tensor(missed[:, 4:5], missed[:, 1:2], found_l[:, :], ALU.add))
            st.did(nc.vector.tensor_scalar(missed[:, 2:3], missed[:, 0:1], 0.5, float(TILES * N // 2), ALU.mult, ALU.add))
            st.wait()
            nc.vector.tensor_tensor(missed[:, 3:4], missed[:, 2:3], missed[:, 4:5], ALU.subtract
                                    ).then_inc(missed_ready, 1)
            dve.wait_ge(redo_psum, 1)
            nc.vector.tensor_scalar(redo_i[:, :], ps_cnt[0:1, 4 * RANKS:4 * RANKS + 1], 0.0, None, ALU.is_gt
                                    ).then_inc(redo_ready, 1)

            with dve.If(must_redo(dve)):
                st.did(nc.vector.tensor_copy(cols[:, 0, :], h_all[:, :, TCOL]))
                st.wait()
                nc.vector.tensor_copy(cols[:, 1, :], h_all[:, :, FCOL]).then_inc(cols_ready, 1)
                dve.wait_ge(rows_psum, 1)
                nc.vector.tensor_copy(rows[:, :, :], ps_misc[0:TILES, 0:2 * P].rearrange("c (r p) -> c r p", p=P)
                                      ).then_inc(rows_ready, 1)
                dve.wait_ge(rows_landed, 32)
                dve.sem_inc(d_free, 1)
                st.restart()
                with dve.Fori(0, TILES) as t:
                    def step(ins):
                        st.did(ins)
                        st.wait()

                    dve.wait_ge(d_adj_landed, 16 * (t + 1))
                    step(nc.vector.scalar_tensor_tensor(out=d_valid, in0=d_adj, scalar=0.0, in1=flag_row,
                                                        op0=ALU.is_gt, op1=ALU.mult))
                    step(nc.vector.reduce_sum(one[:, 0:1], d_valid, AX_X))
                    step(nc.vector.tensor_scalar(d_valid, d_valid, BIG, -BIG, ALU.mult, ALU.add))
                    step(nc.vector.tensor_tensor(d_att, d_valid, t_row, ALU.add))
                    step(nc.vector.reduce_max(one[:, 1:2], d_att, AX_X))
                    step(nc.vector.tensor_copy(one[:, 2:3], s_all[:, bass.ds(t, 1)]))
                    step(nc.vector.tensor_tensor(one[:, 3:4], one[:, 1:2], one[:, 2:3], ALU.add))
                    step(nc.vector.scalar_tensor_tensor(out=one[:, 1:2], in0=one[:, 3:4], scalar=ALPHA,
                                                        in1=one[:, 3:4], op0=ALU.mult, op1=ALU.max))
                    step(nc.vector.tensor_scalar(one[:, 3:4], one[:, 1:2], FLOOR, None, ALU.max))
                    step(nc.vector.tensor_scalar(one[:, 4:5], one[:, 3:4], -1.0, None, ALU.mult))
                    step(nc.vector.tensor_scalar(d_att, d_att, one[:, 2:3], None, ALU.add))
                    nc.vector.scalar_tensor_tensor(out=d_att, in0=d_att, scalar=ALPHA, in1=d_att,
                                                   op0=ALU.mult, op1=ALU.max).then_inc(d_score_ready, 1)
                    dve.wait_ge(d_prob_ready, t + 1)
                    step(nc.vector.tensor_scalar(one[:, 6:7], one[:, 5:6], 1.0 / BIG, None, ALU.max))
                    step(nc.vector.reciprocal(one[:, 7:8], one[:, 6:7]))
                    step(nc.vector.scalar_tensor_tensor(out=one[:, 8:9], in0=one[:, 7:8], scalar=THR, in1=one[:, 0:1],
                                                        op0=ALU.is_gt, op1=ALU.mult))
                    step(nc.vector.tensor_scalar(d_att, d_att, one[:, 7:8], None, ALU.mult))
                    nc.vector.scalar_tensor_tensor(out=d_att, in0=d_att, scalar=THR, in1=d_att,
                                                   op0=ALU.is_ge, op1=ALU.mult).then_inc(d_att_ready, 1)
                    with dve.Fori(0, GROUPS_D) as g:
                        dve.wait_ge(d_T_psum, GROUPS_D * t + g + 2)
                        nc.vector.tensor_copy(attT, ps_DT).then_inc(d_T_ready, 1)
                    dve.wait_ge(d_acc_psum, GROUPS_D * (t + 1))
                    step(nc.vector.scalar_tensor_tensor(
                        out=zacc[:, 0, :], in0=ps_acc, scalar=one[:, 8:9],
                        in1=h_all[:, bass.ds(t, 1), 0:D].rearrange("p a d -> p (a d)"), op0=ALU.mult, op1=ALU.add))
                    nc.vector.tensor_scalar(neg[:, 0, :], zacc[:, 0, :], 0.0, None, ALU.min).then_inc(d_neg_ready, 1)
                    dve.wait_ge(d_eneg_ready, t + 1)
                    step(nc.vector.scalar_tensor_tensor(out=rsum[:, 0, :], in0=zacc[:, 0, :], scalar=0.0,
                                                        in1=eneg[:, 0, :], op0=ALU.max, op1=ALU.add))
                    dve.wait_ge(d_x_landed, 16 * (t + 1))
                    nc.vector.scalar_tensor_tensor(out=ob[:, 0, 0, :], in0=rsum[:, 0, :], scalar=-1.0,
                                                   in1=xr[:, 0, 0, :], op0=ALU.add, op1=ALU.add
                                                   ).then_inc(d_out_ready, 1)
                    dve.wait_ge(d_stored, 16 * (t + 1))
                    dve.sem_inc(d_free, 1)
                    st.restart()


_INS = ["x", "adj", "L0_gnn_W", "L0_gnn_a"]


def kernel(**inputs):
    import numpy as _np
    import concourse.bacc as _bacc
    from concourse import mybir as _mybir
    from concourse.bass_utils import run_bass_kernel_spmd as _run

    nc = _bacc.Bacc("TRN2", target_bir_lowering=False, num_devices=1)
    arrays, args = {}, []
    for name in _INS:
        v = _np.ascontiguousarray(inputs[name])
        arrays[f"in_{name}_dram"] = v
        args.append(nc.dram_tensor(f"in_{name}_dram", v.shape, _mybir.dt.from_np(v.dtype), kind="ExternalInput").ap())
    n, d = inputs["x"].shape
    out = nc.dram_tensor("out_0_dram", (n, d), _mybir.dt.float32, kind="ExternalOutput").ap()
    table = nc.dram_tensor("table_dram", (n, d + 4), _mybir.dt.float32, kind="Internal").ap()
    trow = nc.dram_tensor("trow_dram", (2, n), _mybir.dt.float32, kind="Internal").ap()
    gat_kernel(nc, *args, out, table, trow)
    r = _run(nc, [arrays], core_ids=[0])
    return r.results[0]["out_0_dram"]
```

```python
from contextlib import ExitStack

import concourse.bass as bass
from concourse import mybir

F32 = mybir.dt.float32
BF16 = mybir.dt.bfloat16
I32 = mybir.dt.int32
ALU = mybir.AluOpType
ACT = mybir.ActivationFunctionType
AX_X = mybir.AxisListType.X

P = 128
EPS = 1e-5
THR = 1e-4
ALPHA = 0.2
BIG = 1e30
FLOOR = -1e29

BITS = 8
SEG = 128
SLOTS = 16
DIRECT = 5
RANKS = SLOTS - DIRECT
LISTS = 1
CHUNKS = 2
XPARTS = 8
UNIT = 4


class Steps:

    def __init__(self, eng, sem):
        self.eng, self.sem, self.n = eng, sem, 0

    def did(self, ins):
        self.n += 1
        ins.then_inc(self.sem, 1)

    def wait(self, back=0):
        self.eng.wait_ge(self.sem, self.n - back)

    def restart(self):
        self.wait()
        self.eng.sem_clear(self.sem)
        self.n = 0


def wait_alone(eng, sem, value, waits):
    eng.wait_ge(sem, value)
    eng.sem_inc(waits, 1)


def gat_kernel(nc, x, adj, W, a, out, table, trow):
    N, D = x.shape
    TILES = N // P
    PAIRS = TILES // 2
    GROUPS = N // BITS
    NSEG = GROUPS // SEG
    CW = N // CHUNKS
    TW = table.shape[1]
    TCOL, FCOL, SCOL = D, D + 1, D + 2
    PART = TILES // XPARTS
    UNITS = TILES // UNIT
    BIAS = float((2 ** BITS - 1) * GROUPS // 2)
    S2 = 2 * SLOTS
    WIN = LISTS * P + RANKS
    NL = 2 * LISTS
    NG = 2 * DIRECT + NL

    x_t = x.rearrange("(t p) d -> p t d", p=P)
    out_t = out.rearrange("(t p) d -> p t d", p=P)
    adj_t = adj.rearrange("(t p) j -> p t j", p=P)
    table_t = table.rearrange("(t p) d -> p t d", p=P)

    with ExitStack() as ctx:
        def sb(name, shape, dt):
            return ctx.enter_context(nc.sbuf_tensor(name, shape, dt))

        def ps(name, shape, dt):
            return ctx.enter_context(nc.psum_tensor(name, shape, dt))

        def sem(name):
            return ctx.enter_context(nc.semaphore(name))

        adj_sb = sb("adj_sb", [P, 2 * CHUNKS, CW], I32)
        mask = sb("mask", [P, 2 * CHUNKS, CW], BF16)
        x_all = sb("x_all", [P, TILES, D], F32)
        h_all = sb("h_all", [P, TILES, TW], F32)
        scratch = sb("scratch", [P, max(2 * NG * TW + (NL + 3 * 2) * D, 4 * PART * D)], F32)
        xc, sq = [scratch[:, 2 * v * PART * D:2 * (v + 1) * PART * D].rearrange("p (a t d) -> p a t d", a=2, d=D)
                  for v in range(2)]
        gath = scratch[:, 0:2 * NG * TW].rearrange("p (a s c) -> p a s c", a=2, c=TW)
        scaled = scratch[:, 2 * NG * TW:2 * NG * TW + NL * D].rearrange("p (l d) -> p l d", d=D)
        elu_at = 2 * NG * TW + NL * D
        zacc, neg, eneg = [
            scratch[:, elu_at + v * 2 * D:elu_at + (v + 1) * 2 * D].rearrange("p (t d) -> p t d", d=D)
            for v in range(3)]

        d_adj = adj_sb[:, 0:CHUNKS, :].rearrange("p c w -> p (c w)")
        d_valid = d_adj.bitcast(F32)
        d_att = adj_sb[:, CHUNKS:2 * CHUNKS, :].rearrange("p c w -> p (c w)").bitcast(F32)
        t_row = mask[:, :, :].rearrange("p c w -> p (c w)").bitcast(F32)
        flag_row = x_all[:, :, :].rearrange("p t d -> p (t d)")
        cols = sb("cols", [P, 2, TILES], F32)
        rows = sb("rows", [TILES, 2, P], F32)
        one = sb("one", [P, 10], F32)
        missed = sb("missed", [P, 6], F32)
        redo_i = sb("redo_i", [1, 1], I32)

        ident = sb("ident", [P, P], F32)
        pack_w = sb("pack_w", [P, BITS, P], BF16)
        ones_b = sb("ones_b", [P, P], BF16)
        word_no = sb("word_no", [P, GROUPS], BF16)
        bit_mask = sb("bit_mask", [P, BITS], I32)
        bit_base = sb("bit_base", [P, BITS], I32)

        before = sb("before", [P, P], BF16)
        win_no = sb("win_no", [P, WIN], BF16)
        count = sb("count", [P, P], F32)
        row_rank = sb("row_rank", [P, 2, RANKS, 2], BF16)
        ones_f = sb("ones_f", [P, 1], F32)
        minus_half = sb("minus_half", [P, 1], F32)

        w_ext = sb("w_ext", [P, D + 3], F32)
        wT = sb("wT", [P, D], F32)
        a3 = sb("a3", [P, 3], F32)
        reluT = sb("reluT", [P, 2, UNIT, P], F32)
        s_all = sb("s_all", [P, TILES], F32)
        mean = sb("mean", [P, TILES], F32)
        var = sb("var", [P, TILES], F32)
        std = sb("std", [P, TILES], F32)
        rstd = sb("rstd", [P, TILES], F32)
        sum1 = sb("sum1", [P, TILES], F32)

        cand = sb("cand", [P, 2, NSEG * 8], F32)
        cand2 = sb("cand2", [P, 2, NSEG * 8], F32)
        words = sb("words", [P, S2], F32)
        words_i = sb("words_i", [P, S2], I32)
        word_n = sb("word_n", [P, S2], I32)
        bits = sb("bits", [P, S2, BITS], I32)
        keyf = sb("keyf", [P, S2, BITS], F32)
        ekey = sb("ekey", [P, S2, BITS], F32)
        ekey2 = sb("ekey2", [P, S2, BITS], F32)
        keys = sb("keys", [P, 2, S2], F32)
        idx = sb("idx", [P, 2, NG], I32)
        has = sb("has", [P, 2, SLOTS], BF16)
        extra = sb("extra", [P, 2], BF16)
        feat = sb("feat", [P, 2, RANKS, 4], BF16)
        place = sb("place", [P, 2, 2, WIN], BF16)
        entry = sb("entry", [P, 2, NL, 4], F32)
        entry_key = sb("entry_key", [P, NL], F32)
        used = sb("used", [P, 2, NL], F32)
        found = sb("found", [P, 2, DIRECT], F32)
        found_in_lists = sb("found_in_lists", [P, NL], F32)
        sgn_sum = sb("sgn_sum", [P, TILES * CHUNKS], F32)

        t_flag = sb("t_flag", [P, NL, 2], F32)
        owner = sb("owner", [P, NL, P], F32)
        at_rank = sb("at_rank", [P, NL, RANKS], F32)
        by_rank = sb("by_rank", [P, NL, 2, RANKS], F32)
        valid = sb("valid", [P, S2], F32)
        t_s = sb("t_s", [P, S2], F32)
        w_rest = sb("w_rest", [P, 2, RANKS], F32)
        w_parts = sb("w_parts", [P, 2, RANKS, 3], BF16)
        w_entry = sb("w_entry", [P, NL], F32)
        deg = sb("deg", [P, 2], F32)
        tm = sb("tm", [P, S2], F32)
        tm2 = sb("tm2", [P, S2], F32)
        mx = sb("mx", [P, 2], F32)
        sc = sb("sc", [P, 3, S2], F32)
        prob = sb("prob", [P, S2], F32)
        zz = sb("zz", [P, 4, 2], F32)
        att = sb("att", [P, 3, S2], F32)
        ob = sb("ob", [P, 2, 2, D], F32)

        ps_words = [ps(f"ps_words{i}", [P, GROUPS], F32) for i in range(2)]
        ps_T = [ps(f"ps_T{i}", [P, UNIT, P], F32) for i in range(2)]
        ps_back = ps("ps_back", [P, 512], F32)
        ps_misc = ps("ps_misc", [P, 512], F32)
        ps_H = [ps_words[i][:, :].rearrange("p (t c) -> p t c", t=UNIT)[:, :, 0:D + 3] for i in range(2)]

        ps_first = ps_T[0][:, 0, 0:2]
        ps_entry = ps_T[1][:, 0, 0:4 * NL].rearrange("p (l c) -> p l c", c=4)
        ps_t = ps_back[:, 0:4 * RANKS].rearrange("p (t v r) -> p t v r", t=2, v=2)
        ps_sum = ps_misc[:, 0:2 * D].rearrange("p (t d) -> p t d", d=D)
        ps_w = ps_misc[:, 2 * D:2 * D + 3 * NL].rearrange("p (l c) -> p l c", c=3)

        const_ready = sem("const_ready")
        pool_steps = sem("pool_steps")
        pool_waits = sem("pool_waits")
        dve_steps = sem("dve_steps")
        dve_waits = sem("dve_waits")
        x_landed = [sem(f"x_landed{i}") for i in range(XPARTS)]
        w_landed = sem("w_landed")
        adj_landed = [sem(f"adj_landed{i}") for i in range(2 * CHUNKS)]
        xc_ready = sem("xc_ready")
        sq_ready = sem("sq_ready")
        var_ready = sem("var_ready")
        std_ready = sem("std_ready")
        wT_psum = sem("wT_psum")
        wT_ready = sem("wT_ready")
        we_psum = sem("we_psum")
        we_ready = sem("we_ready")
        reluT_psum = sem("reluT_psum")
        reluT_ready = sem("reluT_ready")
        h_psum = sem("h_psum")
        h_ready = sem("h_ready")
        part_ready = sem("part_ready")
        table_stored = sem("table_stored")
        mask_ready = sem("mask_ready")
        mask_used = sem("mask_used")
        words_ready = sem("words_ready")
        words_used = sem("words_used")
        idx_ready = sem("idx_ready")
        extra_ready = sem("extra_ready")
        first_psum = sem("first_psum")
        place_ready = sem("place_ready")
        entry_psum = sem("entry_psum")
        list_ready = sem("list_ready")
        by_rank_ready = sem("by_rank_ready")
        t_psum = sem("t_psum")
        w_ready = sem("w_ready")
        w_psum = sem("w_psum")
        scaled_ready = sem("scaled_ready")
        sum_psum = sem("sum_psum")
        gathered = [sem(f"gathered{i}") for i in range(2)]
        score_ready = sem("score_ready")
        prob_ready = sem("prob_ready")
        neg_ready = sem("neg_ready")
        eneg_ready = sem("eneg_ready")
        out_ready = sem("out_ready")
        out_stored = [sem(f"out_stored{i}") for i in range(2)]

        missed_ready = sem("missed_ready")
        redo_psum = sem("redo_psum")
        redo_ready = sem("redo_ready")
        cols_ready = sem("cols_ready")
        rows_psum = sem("rows_psum")
        rows_ready = sem("rows_ready")
        rows_stored = sem("rows_stored")
        rows_landed = sem("rows_landed")
        d_free = sem("d_free")
        d_adj_landed = sem("d_adj_landed")
        d_x_landed = sem("d_x_landed")
        d_score_ready = sem("d_score_ready")
        d_prob_ready = sem("d_prob_ready")
        d_att_ready = sem("d_att_ready")
        d_stage_ready = sem("d_stage_ready")
        d_T_psum = sem("d_T_psum")
        d_T_ready = sem("d_T_ready")
        d_acc_psum = sem("d_acc_psum")
        d_neg_ready = sem("d_neg_ready")
        d_eneg_ready = sem("d_eneg_ready")
        d_out_ready = sem("d_out_ready")
        d_stored = sem("d_stored")
        GROUPS_D = TILES // UNIT
        stage, attT = scratch[:, 0:UNIT * D].rearrange("p (t d) -> p t d", d=D), reluT[:, 0, :, :]
        d_x = scratch[:, UNIT * D:(UNIT + 1) * D].rearrange("p (a d) -> p a d", a=1)
        ps_DT = ps_T[0][:, :, :]
        ps_acc = ps_words[1][:, 0:D]

        def must_redo(eng):
            eng.wait_ge(redo_ready, 1)
            return eng.value_load(redo_i[0:1, 0:1], min_val=0, max_val=1) > 0

        block = ctx.enter_context(nc.Block())

        @block.sync
        def _(sp):
            def load_adj(i, par):
                q = 2 * i + par
                for b in range(2 * CHUNKS):
                    ti, c = b // CHUNKS, b % CHUNKS
                    if not (isinstance(q, int) and q == 0):
                        sp.wait_ge(mask_ready, 2 * CHUNKS * q + (b + 1 - 2 * CHUNKS))
                    sp.dma_start(adj_sb[:, b, :], adj_t[:, bass.ds(2 * q + ti, 1), c * CW:(c + 1) * CW]
                                 ).then_inc(adj_landed[b], 16)

            def store(i, par):
                q = 2 * i + par
                sp.wait_ge(out_ready, q + 1)
                sp.dma_start(out_t[:, bass.ds(2 * q, 2), :], ob[:, par, :, :]).then_inc(out_stored[par], 16)

            for k in range(XPARTS):
                sp.dma_start(x_all[:, k * PART:(k + 1) * PART, :], x_t[:, k * PART:(k + 1) * PART, :]
                             ).then_inc(x_landed[k], 16)
                if k == 0:
                    sp.dma_start(w_ext[:, 0:D], W).then_inc(w_landed, 16)
                    sp.dma_start(a3[:, 0:1], a[D:2 * D, :]).then_inc(w_landed, 16)
                    sp.dma_start(a3[:, 2:3], a[0:D, :]).then_inc(w_landed, 16)
            for i in range(2):
                for par in range(2):
                    load_adj(i, par)
            with sp.Fori(2, PAIRS // 2) as i:
                for par in range(2):
                    load_adj(i, par)
                    store(i - 2, par)
            for i in (PAIRS // 2 - 2, PAIRS // 2 - 1):
                for par in range(2):
                    store(i, par)
            for par in range(2):
                sp.wait_ge(out_stored[par], 16 * (PAIRS // 2))

            with sp.If(must_redo(sp)):
                sp.wait_ge(rows_ready, 1)
                for r in range(2):
                    sp.dma_start(trow[r:r + 1, :].rearrange("a (c p) -> (a c) p", p=P), rows[:, r, :]
                                 ).then_inc(rows_stored, 16)
                sp.wait_ge(rows_stored, 32)
                sp.dma_start(t_row, trow[0:1, :].to_broadcast([P, N])).then_inc(rows_landed, 16)
                sp.dma_start(flag_row, trow[1:2, :].to_broadcast([P, N])).then_inc(rows_landed, 16)
                with sp.Fori(0, TILES) as t:
                    sp.wait_ge(d_free, t + 1)
                    sp.dma_start(d_adj, adj_t[:, bass.ds(t, 1), :].rearrange("p a j -> p (a j)")
                                 ).then_inc(d_adj_landed, 16)
                    sp.dma_start(d_x, x_t[:, bass.ds(t, 1), :]).then_inc(d_x_landed, 16)
                    sp.wait_ge(d_out_ready, t + 1)
                    sp.dma_start(out_t[:, bass.ds(t, 1), :], ob[:, 0, 0:1, :]).then_inc(d_stored, 16)
                sp.wait_ge(d_stored, 16 * TILES)

        @block.gpsimd
        def _(pool):
            st = Steps(pool, pool_steps)

            def made(ins):
                st.did(ins)
                st.wait()

            made(nc.gpsimd.memset(a3[:, 1:2], 1.0))
            made(nc.gpsimd.memset(ident[:, :], 0.0))
            made(nc.gpsimd.affine_select(out=ident[:, :], in_=ident[:, :], compare_op=ALU.not_equal, fill=1.0,
                                         base=0, pattern=[[-1, P]], channel_multiplier=1))
            made(nc.gpsimd.memset(minus_half[:, :], -0.5))
            pool.sem_inc(const_ready, 1)
            made(nc.gpsimd.memset(pack_w[:, :, :], 0.0))
            for b in range(BITS):
                made(nc.gpsimd.affine_select(out=pack_w[:, b, :], in_=pack_w[:, b, :], compare_op=ALU.not_equal,
                                             fill=float(2 ** b * GROUPS // 2), base=0, pattern=[[-1, P]],
                                             channel_multiplier=1))
            made(nc.gpsimd.memset(ones_b[:, :], 1.0))
            made(nc.gpsimd.memset(word_no[:, :], 0.0))
            hi = GROUPS // P
            made(nc.gpsimd.iota(word_no[0:1, :].rearrange("p (h l) -> p h l", l=P), [[-P, hi], [0, P]],
                                base=GROUPS - P, channel_multiplier=0, allow_small_or_imprecise_dtypes=True))
            made(nc.gpsimd.iota(word_no[32:33, :].rearrange("p (h l) -> p h l", l=P), [[0, hi], [-1, P]],
                                base=P - 1, channel_multiplier=0, allow_small_or_imprecise_dtypes=True))
            for b in range(BITS):
                made(nc.gpsimd.memset(bit_mask[:, b:b + 1], GROUPS * 2 ** b))
            made(nc.gpsimd.iota(bit_base[:, :], [[-GROUPS, BITS]], base=1 + GROUPS * (BITS - 1),
                                channel_multiplier=0))
            made(nc.gpsimd.memset(before[:, :], 1.0))
            made(nc.gpsimd.affine_select(out=before[:, :], in_=before[:, :], compare_op=ALU.is_gt, fill=0.0,
                                         base=0, pattern=[[1, P]], channel_multiplier=-1))
            made(nc.gpsimd.iota(win_no[:, :], [[1, WIN]], base=-RANKS, channel_multiplier=0,
                                allow_small_or_imprecise_dtypes=True))
            made(nc.gpsimd.iota(count[:, :], [[1, P]], base=0, channel_multiplier=0,
                                allow_small_or_imprecise_dtypes=True))
            made(nc.gpsimd.iota(row_rank[:, :, :, 0], [[0, 2], [0, RANKS]], base=0, channel_multiplier=1,
                                allow_small_or_imprecise_dtypes=True))
            made(nc.gpsimd.iota(row_rank[:, :, :, 1], [[0, 2], [1, RANKS]], base=0, channel_multiplier=0,
                                allow_small_or_imprecise_dtypes=True))
            made(nc.gpsimd.memset(ones_f[:, :], 1.0))
            made(nc.gpsimd.memset(h_all[:, :, SCOL + 1:TW], 0.0))
            pool.sem_inc(const_ready, 1)

            def gather(par, s):
                nc.gpsimd.indirect_dma_start(
                    gath[:, par, s, :], None, table[:, :],
                    bass.IndirectOffsetOnAxis(ap=idx[:, par, s:s + 1], axis=0),
                    bounds_check=N - 1, oob_is_err=False).then_inc(gathered[par], 16)

            def pair(i, par):
                q = 2 * i + par
                if not (isinstance(i, int) and i == 0):
                    pool.wait_ge(scaled_ready, q - 1)
                for s in range(2 * DIRECT):
                    if s % DIRECT == 0:
                        wait_alone(pool, idx_ready, 2 * q + s // DIRECT + 1, pool_waits)
                    gather(par, s)
                wait_alone(pool, list_ready, q + 1, pool_waits)
                for s in range(2 * DIRECT, NG):
                    gather(par, s)

            for k in range(XPARTS):
                pool.wait_ge(part_ready, k + 1)
                pool.dma_start(table_t[:, k * PART:(k + 1) * PART, :], h_all[:, k * PART:(k + 1) * PART, :]
                               ).then_inc(table_stored, 16)
            pool.wait_ge(table_stored, 16 * XPARTS)
            pair(0, 0)
            pair(0, 1)
            with pool.Fori(1, PAIRS // 2) as i:
                pair(i, 0)
                pair(i, 1)

        @block.scalar
        def _(act):
            def square(k):
                act.wait_ge(xc_ready, k + 1)
                if k >= 2:
                    act.wait_ge(var_ready, k - 1)
                nc.scalar.activation(sq[:, k % 2, :, :], xc[:, k % 2, :, :],
                                     ACT.Square).then_inc(sq_ready, 1)

            def root(k):
                part = slice(k * PART, (k + 1) * PART)
                act.wait_ge(var_ready, k + 1)
                nc.scalar.activation(std[:, part], var[:, part], ACT.Sqrt).then_inc(std_ready, 1)

            def relu(units):
                for u in units:
                    act.wait_ge(reluT_psum, u + 1)
                    if u >= 2:
                        act.wait_ge(h_psum, u - 1)
                    nc.scalar.activation(reluT[:, u % 2, :, :], ps_T[u % 2][:, :, :],
                                         ACT.Relu).then_inc(reluT_ready, 1)

            def cast(i, par, b):
                q = 2 * i + par
                act.wait_ge(adj_landed[b], 16 * (q + 1))
                if not (isinstance(q, int) and q == 0):
                    act.wait_ge(mask_used, 2 * CHUNKS * q + (b + 1 - 2 * CHUNKS))
                nc.scalar.activation(mask[:, b, :], adj_sb[:, b, :], ACT.Sign, bias=minus_half[:, 0:1],
                                     accum_out=sgn_sum[:, bass.ds(2 * CHUNKS * q + b, 1)]
                                     ).then_inc(mask_ready, 1)

            def exp_scores(q):
                act.wait_ge(score_ready, q + 1)
                nc.scalar.activation(prob[:, :], sc[:, 2, :], ACT.Exp, scale=-1.0).then_inc(prob_ready, 1)

            def exp_neg(q):
                act.wait_ge(neg_ready, q + 1)
                nc.scalar.activation(eneg[:, :, :], neg[:, :, :], ACT.Exp).then_inc(eneg_ready, 1)

            def pair(i, par, lag):
                q = 2 * i + par
                cast(i, par, 0)
                cast(i, par, 1)
                if lag >= 3:
                    exp_neg(q - 3)
                cast(i, par, 2)
                if lag >= 2:
                    exp_scores(q - 2)
                cast(i, par, 3)

            square(0)
            for k in range(XPARTS):
                relu(range(UNITS // XPARTS * k, UNITS // XPARTS * (k + 1)))
                if k + 1 < XPARTS:
                    square(k + 1)
                root(k)
                if k == 3:
                    act.wait_ge(const_ready, 1)
                if k >= 3 and k - 3 < 2 * CHUNKS:
                    cast(0, 0, k - 3)
            pair(0, 1, 1)
            pair(1, 0, 2)
            pair(1, 1, 3)
            with act.Fori(2, PAIRS // 2) as i:
                pair(i, 0, 3)
                pair(i, 1, 3)
            exp_neg(PAIRS - 3)
            exp_scores(PAIRS - 2)
            exp_neg(PAIRS - 2)
            exp_scores(PAIRS - 1)
            exp_neg(PAIRS - 1)

            with act.If(must_redo(act)):
                with act.Fori(0, TILES) as t:
                    act.wait_ge(d_score_ready, t + 1)
                    nc.scalar.activation(d_att, d_att, ACT.Exp, bias=one[:, 4:5], accum_out=one[:, 5:6]
                                         ).then_inc(d_prob_ready, 1)
                    act.wait_ge(d_att_ready, t + 1)
                    with act.Fori(0, GROUPS_D) as g:
                        act.wait_ge(d_T_psum, GROUPS_D * t + g + 1)
                        nc.scalar.copy(stage.rearrange("p t d -> p (t d)"), d_att[:, bass.ds(UNIT * P * g, UNIT * P)]
                                       ).then_inc(d_stage_ready, 1)
                    act.wait_ge(d_neg_ready, t + 1)
                    nc.scalar.activation(eneg[:, 0, :], neg[:, 0, :], ACT.Exp).then_inc(d_eneg_ready, 1)

        @block.tensor
        def _(pe):
            pe.wait_ge(const_ready, 1)
            pe.wait_ge(w_landed, 48)
            nc.tensor.transpose(ps_misc[:, 0:D], w_ext[:, 0:D], ident[:, :]).then_inc(wT_psum, 1)
            pe.wait_ge(wT_ready, 1)
            nc.tensor.matmul(ps_misc[:, D:D + 3], wT[:, :], a3[:, :], start=True, stop=True).then_inc(we_psum, 1)
            pe.wait_ge(we_ready, 1)

            def transposes(u):
                per = UNITS // XPARTS
                k = u // per
                pe.wait_ge(xc_ready, k + 1)
                if u >= 2:
                    pe.wait_ge(reluT_ready, u - 1)
                for t in range(UNIT):
                    last = nc.tensor.transpose(ps_T[u % 2][:, t, :], xc[:, k % 2, UNIT * (u % per) + t, :], ident[:, :])
                last.then_inc(reluT_psum, 1)

            def project(u):
                pe.wait_ge(reluT_ready, u + 1)
                if u >= 2:
                    pe.wait_ge(h_ready, u - 1)
                for t in range(UNIT):
                    last = nc.tensor.matmul(ps_H[u % 2][:, t, :], reluT[:, u % 2, t, :], w_ext[:, :],
                                            start=True, stop=True)
                last.then_inc(h_psum, 1)

            transposes(0)
            for u in range(1, UNITS):
                transposes(u)
                project(u - 1)
            project(UNITS - 1)
            pe.wait_ge(h_ready, UNITS)
            pe.wait_ge(const_ready, 2)

            def pack(i, par, b):
                q, ti, c = 2 * i + par, b // CHUNKS, b % CHUNKS
                per = BITS // CHUNKS
                if c == 0 and not (isinstance(q, int) and q == 0):
                    pe.wait_ge(words_used, 2 * q + ti - 1)
                pe.wait_ge(mask_ready, 2 * CHUNKS * q + b + 1)
                for bit in range(per):
                    for bank in range(GROUPS // 512):
                        last = nc.tensor.matmul(
                            ps_words[ti][:, bank * 512:(bank + 1) * 512], pack_w[:, c * per + bit, :],
                            mask[:, b, bit * GROUPS + bank * 512:bit * GROUPS + (bank + 1) * 512],
                            start=(c == 0 and bit == 0), stop=False)
                last.then_inc(mask_used, 1)
                if c == CHUNKS - 1:
                    for bank in range(GROUPS // 512):
                        last = nc.tensor.matmul(ps_words[ti][:, bank * 512:(bank + 1) * 512], ones_b[:, :],
                                                word_no[:, bank * 512:(bank + 1) * 512], start=False, stop=True)
                    last.then_inc(words_ready, 1)

            def to_lists(out, par, values):
                for v in range(NL):
                    ti, first = v // LISTS, v % LISTS * P
                    for r in range(RANKS):
                        window = place[:, par, ti, first + RANKS - r:first + RANKS - r + P]
                        last = nc.tensor.matmul(out[:, v, :], window, values[:, ti, r, :],
                                                start=r == 0, stop=r == RANKS - 1)
                return last

            def make_list(q, par):
                pe.wait_ge(extra_ready, q + 1)
                nc.tensor.matmul(ps_first, before[:, :], extra[:, :], start=True, stop=True).then_inc(first_psum, 1)
                pe.wait_ge(place_ready, q + 1)
                to_lists(ps_entry, par, feat).then_inc(entry_psum, 1)

            def list_scores(q):
                pe.wait_ge(by_rank_ready, q + 1)
                for v in range(NL):
                    last = nc.tensor.matmul(ps_t[:, v // LISTS, :, :].rearrange("p v r -> p (v r)"), owner[:, v, :],
                                            by_rank[:, v, :, :].rearrange("p v r -> p (v r)"),
                                            start=v % LISTS == 0, stop=v % LISTS == LISTS - 1)
                last.then_inc(t_psum, 1)

            def list_weights(q, par):
                pe.wait_ge(w_ready, q + 1)
                to_lists(ps_w, par, w_parts).then_inc(w_psum, 1)

            def list_sum(q):
                pe.wait_ge(scaled_ready, q + 1)
                for v in range(NL):
                    last = nc.tensor.matmul(ps_sum[:, v // LISTS, :], owner[:, v, :], scaled[:, v, :],
                                            start=v % LISTS == 0, stop=v % LISTS == LISTS - 1)
                last.then_inc(sum_psum, 1)

            def pair(i, par, lag):
                q = 2 * i + par
                pack(i, par, 0)
                if lag >= 1:
                    make_list(q - 1, 1 - par)
                if lag >= 2:
                    list_scores(q - 2)
                pack(i, par, 1)
                pack(i, par, 2)
                if lag >= 2:
                    list_weights(q - 2, par)
                pack(i, par, 3)
                if lag >= 2:
                    list_sum(q - 2)

            pair(0, 0, 0)
            pair(0, 1, 1)
            with pe.Fori(1, PAIRS // 2) as i:
                pair(i, 0, 2)
                pair(i, 1, 2)
            make_list(PAIRS - 1, 1)
            for par in range(2):
                list_scores(PAIRS - 2 + par)
                list_weights(PAIRS - 2 + par, par)
                list_sum(PAIRS - 2 + par)

            pe.wait_ge(missed_ready, 1)
            nc.tensor.matmul(ps_back[0:1, 4 * RANKS:4 * RANKS + 1], ones_f[:, :], missed[:, 3:4], start=True, stop=True
                             ).then_inc(redo_psum, 1)
            with pe.If(must_redo(pe)):
                pe.wait_ge(cols_ready, 1)
                for r in range(2):
                    last = nc.tensor.transpose(ps_misc[0:TILES, r * P:(r + 1) * P], cols[:, r, :], ident[:, :])
                last.then_inc(rows_psum, 1)
                pe.sem_inc(d_T_psum, 1)

                def group(t, g, start, stop):
                    pe.wait_ge(d_stage_ready, GROUPS_D * t + g + 1)
                    for k in range(UNIT):
                        last = nc.tensor.transpose(ps_DT[:, k, :], stage[:, k, :], ident[:, :])
                    last.then_inc(d_T_psum, 1)
                    pe.wait_ge(d_T_ready, GROUPS_D * t + g + 1)
                    for k in range(UNIT):
                        h_block = h_all[:, bass.ds(UNIT * g + k, 1), 0:D].rearrange("p a d -> p (a d)")
                        last = nc.tensor.matmul(
                            ps_acc, attT[:, k, :], h_block,
                            start=start and k == 0, stop=stop and k == UNIT - 1)
                    last.then_inc(d_acc_psum, 1)

                with pe.Fori(0, TILES) as t:
                    group(t, 0, True, False)
                    with pe.Fori(1, GROUPS_D - 1) as g:
                        group(t, g, False, False)
                    group(t, GROUPS_D - 1, False, True)

        @block.vector
        def _(dve):
            st = Steps(dve, dve_steps)
            dve.wait_ge(wT_psum, 1)
            nc.vector.tensor_copy(wT[:, :], ps_misc[:, 0:D]).then_inc(wT_ready, 1)
            dve.wait_ge(we_psum, 1)
            nc.vector.tensor_copy(w_ext[:, D:D + 3], ps_misc[:, D:D + 3]).then_inc(we_ready, 1)

            def centre(k):
                part = slice(k * PART, (k + 1) * PART)
                dve.wait_ge(x_landed[k], 16)
                st.did(nc.vector.reduce_sum(sum1[:, part], x_all[:, part, :], AX_X))
                st.wait()
                st.did(nc.vector.tensor_scalar(mean[:, part], sum1[:, part], 1.0 / D, None, ALU.mult))
                if k >= 2:
                    dve.wait_ge(reluT_psum, UNITS // XPARTS * (k - 1))
                    dve.wait_ge(sq_ready, k - 1)
                st.wait()
                nc.vector.tensor_tensor(xc[:, k % 2, :, :], x_all[:, part, :],
                                        mean[:, part].unsqueeze(2).to_broadcast([P, PART, D]),
                                        ALU.subtract).then_inc(xc_ready, 1)

            def variance(k):
                part = slice(k * PART, (k + 1) * PART)
                dve.wait_ge(sq_ready, k + 1)
                st.did(nc.vector.reduce_sum(sum1[:, part], sq[:, k % 2, :, :], AX_X))
                st.wait()
                nc.vector.tensor_scalar(var[:, part], sum1[:, part], 1.0 / D, EPS, ALU.mult, ALU.add
                                        ).then_inc(var_ready, 1)

            def scale(units):
                for u in units:
                    per = UNITS // XPARTS
                    k, part = u // per, slice(u // per * PART, (u // per + 1) * PART)
                    if u % per == 0:
                        dve.wait_ge(std_ready, k + 1)
                        st.did(nc.vector.reciprocal(rstd[:, part], std[:, part]))
                        st.wait()
                    tiles = slice(UNIT * u, UNIT * (u + 1))
                    dve.wait_ge(h_psum, u + 1)
                    nc.vector.tensor_tensor(h_all[:, tiles, 0:D + 3], ps_H[u % 2],
                                            rstd[:, tiles].unsqueeze(2).to_broadcast([P, UNIT, D + 3]),
                                            ALU.mult).then_inc(h_ready, 1)
                    if u % per == per - 1:
                        dve.wait_ge(h_ready, u + 1)
                        st.did(nc.vector.tensor_copy(s_all[:, part], h_all[:, part, SCOL]))
                        nc.vector.tensor_scalar(h_all[:, part, FCOL], h_all[:, part, FCOL], 0.0, None,
                                                ALU.not_equal).then_inc(part_ready, 1)

            per = UNITS // XPARTS
            centre(0)
            centre(1)
            for k in range(XPARTS):
                variance(k)
                if k + 2 < XPARTS:
                    centre(k + 2)
                scale(range(per * k, per * (k + 1)))
            st.did(nc.vector.memset(found[:, :, :], 0.0))
            st.did(nc.vector.memset(found_in_lists[:, :], 0.0))
            dve.wait_ge(const_ready, 2)

            def per_tile(v):
                return v.unsqueeze(2).to_broadcast([P, 2, SLOTS])

            def by_tile(v):
                return v.rearrange("p (t k) -> p t k", k=SLOTS)

            def top16(out, rest, src, empty):
                st.did(nc.vector.max(out[:, 0:8], src))
                st.wait()
                st.did(nc.vector.match_replace(rest, out[:, 0:8], src, empty))
                st.wait()
                return nc.vector.max(out[:, 8:16], rest)

            def search(i, par, ti):
                wait_alone(dve, words_ready, 2 * (2 * i + par) + ti + 1, dve_waits)
                for s in range(NSEG):
                    st.did(nc.vector.max(cand[:, ti, s * 8:(s + 1) * 8],
                                         ps_words[ti][:, s * SEG:(s + 1) * SEG]))
                st.wait()
                dve.sem_inc(words_used, 1)
                st.did(top16(words[:, ti * SLOTS:(ti + 1) * SLOTS], cand2[:, ti, :], cand[:, ti, :], -BIG))

            def extract(i, par, ti):
                part = slice(ti * SLOTS, (ti + 1) * SLOTS)
                tile = [P, SLOTS, BITS]
                st.wait()
                st.did(nc.vector.tensor_scalar(words_i[:, part], words[:, part], BIAS, None, ALU.add))
                st.wait()
                st.did(nc.vector.tensor_scalar(word_n[:, part], words_i[:, part], GROUPS - 1, None, ALU.bitwise_and))
                st.did(nc.vector.tensor_tensor(bits[:, part, :], words_i[:, part].unsqueeze(2).to_broadcast(tile),
                                               bit_mask[:, :].unsqueeze(1).to_broadcast(tile), ALU.bitwise_and))
                st.wait(1)
                st.did(nc.vector.tensor_tensor(keyf[:, part, :], word_n[:, part].unsqueeze(2).to_broadcast(tile),
                                               bit_base[:, :].unsqueeze(1).to_broadcast(tile), ALU.add))
                st.wait()
                st.did(nc.vector.scalar_tensor_tensor(out=ekey[:, part, :], in0=bits[:, part, :], scalar=0.0,
                                                      in1=keyf[:, part, :], op0=ALU.is_gt, op1=ALU.mult))
                st.wait()
                st.did(top16(keys[:, par, part], ekey2[:, part, :].rearrange("p s b -> p (s b)"),
                             ekey[:, part, :].rearrange("p s b -> p (s b)"), 0.0))
                st.wait()
                key = keys[:, par, part]
                nc.vector.tensor_scalar(idx[:, par, ti * DIRECT:(ti + 1) * DIRECT], key[:, 0:DIRECT],
                                        -1.0, float(N), ALU.mult, ALU.add).then_inc(idx_ready, 1)
                st.did(nc.vector.tensor_scalar(has[:, ti, :], key, 0.0, None, ALU.is_gt))

            def make_list(i, par):
                q = 2 * i + par
                late = by_tile(keys[:, par, :])[:, :, DIRECT:SLOTS]
                st.wait()
                with nc.allow_low_precision(reason="counts up to RANKS are exact in bfloat16"):
                    nc.vector.reduce_sum(extra[:, :], has[:, :, DIRECT:SLOTS], AX_X).then_inc(extra_ready, 1)
                st.did(nc.vector.tensor_copy(feat[:, :, :, 0], late))
                st.did(nc.vector.tensor_tensor(feat[:, :, :, 2:4],
                                               has[:, :, DIRECT:SLOTS].unsqueeze(3).to_broadcast([P, 2, RANKS, 2]),
                                               row_rank[:, :, :, :], ALU.mult))
                st.wait(1)
                st.did(nc.vector.tensor_tensor(feat[:, :, :, 1], late, feat[:, :, :, 0], ALU.subtract))
                st.did(nc.vector.tensor_tensor(found[:, :, :], found[:, :, :], has[:, :, 0:DIRECT], ALU.add))
                dve.wait_ge(first_psum, q + 1)
                st.wait()
                for ti in range(2):
                    last = nc.vector.tensor_scalar(place[:, par, ti, :], win_no[:, :], ps_first[:, ti:ti + 1], None,
                                                   ALU.is_equal)
                last.then_inc(place_ready, 1)
                dve.wait_ge(entry_psum, q + 1)
                st.did(nc.vector.tensor_copy(entry[:, par, :, :], ps_entry))
                st.wait()
                st.did(nc.vector.tensor_tensor(entry_key[:, :], entry[:, par, :, 0], entry[:, par, :, 1], ALU.add))
                st.wait()
                nc.vector.tensor_scalar(idx[:, par, 2 * DIRECT:NG], entry_key[:, :], -1.0, float(N), ALU.mult, ALU.add
                                        ).then_inc(list_ready, 1)
                st.did(nc.vector.tensor_scalar(used[:, par, :], entry_key[:, :], 0.0, None, ALU.is_gt))
                st.wait()
                st.did(nc.vector.tensor_tensor(found_in_lists[:, :], found_in_lists[:, :], used[:, par, :], ALU.add))

            def spread(i, par):
                q = 2 * i + par
                dve.wait_ge(gathered[par], 16 * NG * (i + 1))
                st.did(nc.vector.tensor_tensor(t_flag[:, :, :], gath[:, par, 2 * DIRECT:NG, TCOL:FCOL + 1],
                                               used[:, par, :].unsqueeze(2).to_broadcast([P, NL, 2]), ALU.mult))
                st.did(nc.vector.tensor_tensor(
                    at_rank[:, :, :], count[:, 0:RANKS].unsqueeze(1).to_broadcast([P, NL, RANKS]),
                    entry[:, par, :, 3].unsqueeze(2).to_broadcast([P, NL, RANKS]), ALU.is_equal))
                st.did(nc.vector.tensor_tensor(
                    owner[:, :, :], count[:, :].unsqueeze(1).to_broadcast([P, NL, P]),
                    entry[:, par, :, 2].unsqueeze(2).to_broadcast([P, NL, P]), ALU.is_equal))
                st.wait(1)
                nc.vector.tensor_tensor(
                    by_rank[:, :, :, :], at_rank[:, :, :].unsqueeze(2).to_broadcast([P, NL, 2, RANKS]),
                    t_flag[:, :, :].unsqueeze(3).to_broadcast([P, NL, 2, RANKS]), ALU.mult).then_inc(by_rank_ready, 1)

            def scores(i, par):
                q = 2 * i + par
                s_q = s_all[:, bass.ds(2 * q, 2)]
                slots = gath[:, par, 0:2 * DIRECT, :].rearrange("p (t k) c -> p t k c", k=DIRECT)
                st.did(nc.vector.scalar_tensor_tensor(
                    out=by_tile(valid[:, :])[:, :, 0:DIRECT], in0=by_tile(keys[:, par, :])[:, :, 0:DIRECT], scalar=0.0,
                    in1=slots[:, :, :, FCOL], op0=ALU.is_gt, op1=ALU.mult))
                st.did(nc.vector.tensor_copy(by_tile(t_s[:, :])[:, :, 0:DIRECT], slots[:, :, :, TCOL]))
                dve.wait_ge(t_psum, q + 1)
                st.did(nc.vector.tensor_copy(by_tile(t_s[:, :])[:, :, DIRECT:SLOTS], ps_t[:, :, 0, :]))
                st.did(nc.vector.tensor_copy(by_tile(valid[:, :])[:, :, DIRECT:SLOTS], ps_t[:, :, 1, :]))
                st.wait()
                st.did(nc.vector.tensor_scalar(tm[:, :], valid[:, :], BIG, -BIG, ALU.mult, ALU.add))
                st.did(nc.vector.reduce_sum(deg[:, :], by_tile(valid[:, :]), AX_X))
                st.wait(1)
                st.did(nc.vector.tensor_tensor(tm2[:, :], tm[:, :], t_s[:, :], ALU.add))
                st.wait()
                st.did(nc.vector.tensor_tensor(by_tile(sc[:, 0, :]), by_tile(tm2[:, :]), per_tile(s_q), ALU.add))
                st.wait()
                st.did(nc.vector.scalar_tensor_tensor(out=sc[:, 1, :], in0=sc[:, 0, :], scalar=ALPHA,
                                                      in1=sc[:, 0, :], op0=ALU.mult, op1=ALU.max))
                st.wait()
                st.did(nc.vector.reduce_max(mx[:, :], by_tile(sc[:, 1, :]), AX_X))
                st.wait()
                nc.vector.scalar_tensor_tensor(out=by_tile(sc[:, 2, :]), in0=per_tile(mx[:, :]), scalar=FLOOR,
                                               in1=by_tile(sc[:, 1, :]), op0=ALU.max, op1=ALU.subtract
                                               ).then_inc(score_ready, 1)

            def aggregate(i, par):
                q = 2 * i + par
                dve.wait_ge(prob_ready, q + 1)
                st.did(nc.vector.reduce_sum(zz[:, 0, :], by_tile(prob[:, :]), AX_X))
                st.wait()
                st.did(nc.vector.tensor_scalar(zz[:, 1, :], zz[:, 0, :], 1.0 / BIG, None, ALU.max))
                st.wait()
                st.did(nc.vector.reciprocal(zz[:, 2, :], zz[:, 1, :]))
                st.wait()
                st.did(nc.vector.scalar_tensor_tensor(out=zz[:, 3, :], in0=zz[:, 2, :], scalar=THR, in1=deg[:, :],
                                                      op0=ALU.is_gt, op1=ALU.mult))
                st.did(nc.vector.tensor_tensor(by_tile(att[:, 0, :]), by_tile(prob[:, :]), per_tile(zz[:, 2, :]),
                                               ALU.mult))
                st.wait()
                st.did(nc.vector.scalar_tensor_tensor(out=att[:, 1, :], in0=att[:, 0, :], scalar=THR,
                                                      in1=att[:, 0, :], op0=ALU.is_ge, op1=ALU.mult))
                st.wait()
                st.did(nc.vector.tensor_tensor(by_tile(att[:, 2, :]), by_tile(att[:, 1, :]), per_tile(zz[:, 3, :]),
                                               ALU.mult))
                st.wait()
                late = by_tile(att[:, 2, :])[:, :, DIRECT:SLOTS]
                st.did(nc.vector.tensor_copy(w_parts[:, :, :, 0], late))
                st.wait()
                st.did(nc.vector.tensor_tensor(w_rest[:, :, :], late, w_parts[:, :, :, 0], ALU.subtract))
                st.wait()
                st.did(nc.vector.tensor_copy(w_parts[:, :, :, 1], w_rest[:, :, :]))
                st.wait()
                nc.vector.tensor_tensor(w_parts[:, :, :, 2], w_rest[:, :, :], w_parts[:, :, :, 1], ALU.subtract
                                        ).then_inc(w_ready, 1)
                for k in range(DIRECT):
                    for ti in range(2):
                        if k == 0:
                            so_far = h_all[:, bass.ds(2 * q + ti, 1), 0:D].rearrange("p a d -> p (a d)")
                        else:
                            so_far = zacc[:, ti, :]
                            st.wait(1)
                        st.did(nc.vector.scalar_tensor_tensor(
                            out=zacc[:, ti, :], in0=gath[:, par, ti * DIRECT + k, 0:D],
                            scalar=att[:, 2, ti * SLOTS + k:ti * SLOTS + k + 1],
                            in1=so_far, op0=ALU.mult, op1=ALU.add))
                dve.wait_ge(w_psum, q + 1)
                st.did(nc.vector.reduce_sum(w_entry[:, :], ps_w, AX_X))
                st.wait()
                nc.vector.tensor_tensor(scaled[:, :, :], gath[:, par, 2 * DIRECT:NG, 0:D],
                                        w_entry[:, :].unsqueeze(2).to_broadcast([P, NL, D]), ALU.mult
                                        ).then_inc(scaled_ready, 1)

            def add_list(i, par):
                q = 2 * i + par
                dve.wait_ge(sum_psum, q + 1)
                st.did(nc.vector.tensor_tensor(zacc[:, :, :], zacc[:, :, :], ps_sum, ALU.add))
                st.wait()
                nc.vector.tensor_scalar(neg[:, :, :], zacc[:, :, :], 0.0, None, ALU.min).then_inc(neg_ready, 1)

            def finish(i, par):
                q = 2 * i + par
                dve.wait_ge(eneg_ready, q + 1)
                st.did(nc.vector.scalar_tensor_tensor(out=eneg[:, :, :], in0=zacc[:, :, :], scalar=0.0,
                                                      in1=eneg[:, :, :], op0=ALU.max, op1=ALU.add))
                if not (isinstance(i, int) and i == 0):
                    dve.wait_ge(out_stored[par], 16 * i)
                st.wait()
                nc.vector.scalar_tensor_tensor(out=ob[:, par, :, :], in0=eneg[:, :, :], scalar=-1.0,
                                               in1=x_all[:, bass.ds(2 * q, 2), :], op0=ALU.add, op1=ALU.add
                                               ).then_inc(out_ready, 1)

            def pair(i, par, lag):
                if lag >= 1:
                    extract(i - 1 + par, 1 - par, 1)
                    make_list(i - 1 + par, 1 - par)
                if lag >= 2:
                    spread(i - 1, par)
                    scores(i - 1, par)
                if lag >= 3:
                    finish(i - 2 + par, 1 - par)
                search(i, par, 0)
                if lag >= 2:
                    aggregate(i - 1, par)
                extract(i, par, 0)
                search(i, par, 1)
                if lag >= 2:
                    add_list(i - 1, par)

            pair(0, 0, 0)
            pair(0, 1, 1)
            pair(1, 0, 2)
            pair(1, 1, 3)
            st.restart()
            with dve.Fori(2, PAIRS // 2) as i:
                pair(i, 0, 3)
                pair(i, 1, 3)
                st.restart()
            extract(PAIRS // 2 - 1, 1, 1)
            make_list(PAIRS // 2 - 1, 1)
            for par in range(2):
                spread(PAIRS // 2 - 1, par)
                scores(PAIRS // 2 - 1, par)
                if par == 0:
                    finish(PAIRS // 2 - 2, 1)
                aggregate(PAIRS // 2 - 1, par)
                add_list(PAIRS // 2 - 1, par)
                finish(PAIRS // 2 - 1, par)
            st.restart()

            dve.wait_ge(mask_ready, 2 * CHUNKS * PAIRS)
            st.did(nc.vector.reduce_sum(missed[:, 0:1], sgn_sum[:, :], AX_X))
            st.did(nc.vector.reduce_sum(missed[:, 1:2], found[:, :, :], mybir.AxisListType.XY))
            st.did(nc.vector.reduce_sum(missed[:, 5:6], found_in_lists[:, :], AX_X))
            st.wait()
            st.did(nc.vector.tensor_tensor(missed[:, 4:5], missed[:, 1:2], missed[:, 5:6], ALU.add))
            st.did(nc.vector.tensor_scalar(missed[:, 2:3], missed[:, 0:1], 0.5, float(TILES * N // 2),
                                           ALU.mult, ALU.add))
            st.wait()
            nc.vector.tensor_tensor(missed[:, 3:4], missed[:, 2:3], missed[:, 4:5], ALU.subtract
                                    ).then_inc(missed_ready, 1)
            dve.wait_ge(redo_psum, 1)
            nc.vector.tensor_scalar(redo_i[:, :], ps_back[0:1, 4 * RANKS:4 * RANKS + 1], 0.0, None, ALU.is_gt
                                    ).then_inc(redo_ready, 1)

            with dve.If(must_redo(dve)):
                st.did(nc.vector.tensor_copy(cols[:, 0, :], h_all[:, :, TCOL]))
                st.wait()
                nc.vector.tensor_copy(cols[:, 1, :], h_all[:, :, FCOL]).then_inc(cols_ready, 1)
                dve.wait_ge(rows_psum, 1)
                nc.vector.tensor_copy(rows[:, :, :], ps_misc[0:TILES, 0:2 * P].rearrange("c (r p) -> c r p", p=P)
                                      ).then_inc(rows_ready, 1)
                dve.wait_ge(rows_landed, 32)
                dve.sem_inc(d_free, 1)
                st.restart()
                with dve.Fori(0, TILES) as t:
                    def step(ins):
                        st.did(ins)
                        st.wait()

                    dve.wait_ge(d_adj_landed, 16 * (t + 1))
                    step(nc.vector.scalar_tensor_tensor(out=d_valid, in0=d_adj, scalar=0.0, in1=flag_row,
                                                        op0=ALU.is_gt, op1=ALU.mult))
                    step(nc.vector.reduce_sum(one[:, 0:1], d_valid, AX_X))
                    step(nc.vector.tensor_scalar(d_valid, d_valid, BIG, -BIG, ALU.mult, ALU.add))
                    step(nc.vector.tensor_tensor(d_att, d_valid, t_row, ALU.add))
                    step(nc.vector.reduce_max(one[:, 1:2], d_att, AX_X))
                    step(nc.vector.tensor_copy(one[:, 2:3], s_all[:, bass.ds(t, 1)]))
                    step(nc.vector.tensor_tensor(one[:, 3:4], one[:, 1:2], one[:, 2:3], ALU.add))
                    step(nc.vector.scalar_tensor_tensor(out=one[:, 1:2], in0=one[:, 3:4], scalar=ALPHA,
                                                        in1=one[:, 3:4], op0=ALU.mult, op1=ALU.max))
                    step(nc.vector.tensor_scalar(one[:, 3:4], one[:, 1:2], FLOOR, None, ALU.max))
                    step(nc.vector.tensor_scalar(one[:, 4:5], one[:, 3:4], -1.0, None, ALU.mult))
                    step(nc.vector.tensor_scalar(d_att, d_att, one[:, 2:3], None, ALU.add))
                    nc.vector.scalar_tensor_tensor(out=d_att, in0=d_att, scalar=ALPHA, in1=d_att,
                                                   op0=ALU.mult, op1=ALU.max).then_inc(d_score_ready, 1)
                    dve.wait_ge(d_prob_ready, t + 1)
                    step(nc.vector.tensor_scalar(one[:, 6:7], one[:, 5:6], 1.0 / BIG, None, ALU.max))
                    step(nc.vector.reciprocal(one[:, 7:8], one[:, 6:7]))
                    step(nc.vector.scalar_tensor_tensor(out=one[:, 8:9], in0=one[:, 7:8], scalar=THR, in1=one[:, 0:1],
                                                        op0=ALU.is_gt, op1=ALU.mult))
                    step(nc.vector.tensor_scalar(d_att, d_att, one[:, 7:8], None, ALU.mult))
                    nc.vector.scalar_tensor_tensor(out=d_att, in0=d_att, scalar=THR, in1=d_att,
                                                   op0=ALU.is_ge, op1=ALU.mult).then_inc(d_att_ready, 1)
                    with dve.Fori(0, GROUPS_D) as g:
                        dve.wait_ge(d_T_psum, GROUPS_D * t + g + 2)
                        nc.vector.tensor_copy(attT, ps_DT).then_inc(d_T_ready, 1)
                    dve.wait_ge(d_acc_psum, GROUPS_D * (t + 1))
                    step(nc.vector.scalar_tensor_tensor(
                        out=zacc[:, 0, :], in0=ps_acc, scalar=one[:, 8:9],
                        in1=h_all[:, bass.ds(t, 1), 0:D].rearrange("p a d -> p (a d)"), op0=ALU.mult, op1=ALU.add))
                    nc.vector.tensor_scalar(neg[:, 0, :], zacc[:, 0, :], 0.0, None, ALU.min).then_inc(d_neg_ready, 1)
                    dve.wait_ge(d_eneg_ready, t + 1)
                    step(nc.vector.scalar_tensor_tensor(out=eneg[:, 0, :], in0=zacc[:, 0, :], scalar=0.0,
                                                        in1=eneg[:, 0, :], op0=ALU.max, op1=ALU.add))
                    dve.wait_ge(d_x_landed, 16 * (t + 1))
                    nc.vector.scalar_tensor_tensor(out=ob[:, 0, 0, :], in0=eneg[:, 0, :], scalar=-1.0,
                                                   in1=d_x.rearrange("p a d -> p (a d)"), op0=ALU.add, op1=ALU.add
                                                   ).then_inc(d_out_ready, 1)
                    dve.wait_ge(d_stored, 16 * (t + 1))
                    dve.sem_inc(d_free, 1)
                    st.restart()


_INS = ["x", "adj", "L0_gnn_W", "L0_gnn_a"]


def kernel(**inputs):
    import numpy as _np
    import concourse.bacc as _bacc
    from concourse import mybir as _mybir
    from concourse.bass_utils import run_bass_kernel_spmd as _run

    nc = _bacc.Bacc("TRN2", target_bir_lowering=False, num_devices=1)
    arrays, args = {}, []
    for name in _INS:
        v = _np.ascontiguousarray(inputs[name])
        arrays[f"in_{name}_dram"] = v
        args.append(nc.dram_tensor(f"in_{name}_dram", v.shape, _mybir.dt.from_np(v.dtype), kind="ExternalInput").ap())
    n, d = inputs["x"].shape
    out = nc.dram_tensor("out_0_dram", (n, d), _mybir.dt.float32, kind="ExternalOutput").ap()
    table = nc.dram_tensor("table_dram", (n, d + 4), _mybir.dt.float32, kind="Internal").ap()
    trow = nc.dram_tensor("trow_dram", (2, n), _mybir.dt.float32, kind="Internal").ap()
    gat_kernel(nc, *args, out, table, trow)
    r = _run(nc, [arrays], core_ids=[0])
    return r.results[0]["out_0_dram"]
```
